# Optimizing a Trainium2 kernel written in Bass

```python
import numpy as np
import jax
import jax.numpy as jnp

def _softmax(x, axis=-1):
    return jax.nn.softmax(x, axis=axis)

def _gelu(x):
    return jax.nn.gelu(x, approximate=True)

def _silu(x):
    return jax.nn.silu(x)

def _sigmoid(x):
    return jax.nn.sigmoid(x)

def _layernorm(x, axis=-1, eps=1e-05):
    m = jnp.mean(x, axis=axis, keepdims=True)
    v = jnp.var(x, axis=axis, keepdims=True)
    return (x - m) / jnp.sqrt(v + eps)

def _scatter_add(tgt, idx, src, axis=0):
    return tgt.at[idx].add(src)

def _segment_sum(src, seg, n):
    return jax.ops.segment_sum(src, seg, n)
kernel_name = 'mk_xattn_seq_d2_seqx_r4_93c8c7'

def setup_inputs(seed: int=0):
    np.random.seed(seed)
    _w = jnp.asarray

    def _rec_inputs():
        import jax
        import jax.numpy as jnp
        _rk = jax.random.key(seed)
        x = -0.0001233 + 1 * jax.random.normal(jax.random.fold_in(_rk, 1), (4, 512, 320), jnp.float32)
        _lenS = 512 - jax.random.randint(jax.random.fold_in(_rk, 7), (4,), 0, max(1, 512 // 4) + 1, jnp.int32)
        _lenS2 = 1601 - jax.random.randint(jax.random.fold_in(_rk, 8), (4,), 0, max(1, 1601 // 4) + 1, jnp.int32)
        _ctx_768P = jax.random.normal(jax.random.fold_in(_rk, 11), (4, 16, 192), jnp.float32)
        _ctx_768c = jax.random.dirichlet(jax.random.fold_in(_rk, 511), 0.3 * jnp.ones((16,), jnp.float32), (4, 1601))
        _ctx_768t = jnp.einsum('bsk,bkd->bsd', _ctx_768c, _ctx_768P)
        _ctx_768t = _ctx_768t * jax.lax.rsqrt(jnp.mean(jnp.square(_ctx_768t)) + 1e-12) * 0.953939
        ctx_768 = 0.00272024 + 0.999456 * (_ctx_768t + 0.3 * jax.random.normal(jax.random.fold_in(_rk, 611), (4, 1601, 192), jnp.float32))
        return (x, ctx_768)
    x, ctx_768 = _rec_inputs()

    def _L0_xattn_setup():
        import jax, jax.numpy as jnp
        import numpy as np
        D = 320
        H = 20
        DH = D // H
        CTX = 192
        FF_IN = 4 * D
        EPS = 1e-05

        def _ln(x, g, b):
            m = jnp.mean(x, axis=-1, keepdims=True)
            v = jnp.mean(jnp.square(x - m), axis=-1, keepdims=True)
            return (x - m) * jax.lax.rsqrt(v + EPS) * g + b

        def _attn(x, ctx, wq, wk, wv, wo, bo, heads):
            b, n, _ = x.shape
            j = ctx.shape[1]
            dh = wq.shape[1] // heads
            scale = dh ** (-0.5)
            q = (x @ wq).reshape(b, n, heads, dh).transpose(0, 2, 1, 3)
            k = (ctx @ wk).reshape(b, j, heads, dh).transpose(0, 2, 1, 3)
            v = (ctx @ wv).reshape(b, j, heads, dh).transpose(0, 2, 1, 3)
            sim = jnp.einsum('bhid,bhjd->bhij', q, k) * scale
            a = jax.nn.softmax(sim, axis=-1)
            out = jnp.einsum('bhij,bhjd->bhid', a, v)
            out = out.transpose(0, 2, 1, 3).reshape(b, n, heads * dh)
            return out @ wo + bo
        key = jax.random.key(seed)
        ks = jax.random.split(key, 24)
        r = lambda k, shp, s: jax.random.normal(k, shp, dtype=jnp.float32) * s
        d = {'x': r(ks[0], (8, 256, D), 1.0), 'context': r(ks[1], (8, 77, CTX), 1.0), 'heads': H, 'n1_g': jnp.ones((D,), jnp.float32), 'n1_b': jnp.zeros((D,), jnp.float32), 'q1': r(ks[2], (D, D), D ** (-0.5)), 'k1': r(ks[3], (D, D), D ** (-0.5)), 'v1': r(ks[4], (D, D), D ** (-0.5)), 'o1_w': r(ks[5], (D, D), D ** (-0.5)), 'o1_b': jnp.zeros((D,), jnp.float32), 'n2_g': jnp.ones((D,), jnp.float32), 'n2_b': jnp.zeros((D,), jnp.float32), 'q2': r(ks[6], (D, D), D ** (-0.5)), 'k2': r(ks[7], (CTX, D), CTX ** (-0.5)), 'v2': r(ks[8], (CTX, D), CTX ** (-0.5)), 'o2_w': r(ks[9], (D, D), D ** (-0.5)), 'o2_b': jnp.zeros((D,), jnp.float32), 'n3_g': jnp.ones((D,), jnp.float32), 'n3_b': jnp.zeros((D,), jnp.float32), 'ff_w1': r(ks[10], (D, 2 * FF_IN), D ** (-0.5)), 'ff_b1': jnp.zeros((2 * FF_IN,), jnp.float32), 'ff_w2': r(ks[11], (FF_IN, D), FF_IN ** (-0.5)), 'ff_b2': jnp.zeros((D,), jnp.float32)}
        return d
    _L0_xattn_all = _L0_xattn_setup()
    _L0_xattn_in = {k: v for k, v in _L0_xattn_all.items() if k in ('n1_g', 'n1_b', 'q1', 'k1', 'v1', 'o1_w', 'o1_b', 'n2_g', 'n2_b', 'q2', 'k2', 'v2', 'o2_w', 'o2_b', 'n3_g', 'n3_b', 'ff_w1', 'ff_b1', 'ff_w2', 'ff_b2')}
    del _L0_xattn_all

    def _L1_xattn_setup():
        import jax, jax.numpy as jnp
        import numpy as np
        D = 320
        H = 20
        DH = D // H
        CTX = 192
        FF_IN = 4 * D
        EPS = 1e-05

        def _ln(x, g, b):
            m = jnp.mean(x, axis=-1, keepdims=True)
            v = jnp.mean(jnp.square(x - m), axis=-1, keepdims=True)
            return (x - m) * jax.lax.rsqrt(v + EPS) * g + b

        def _attn(x, ctx, wq, wk, wv, wo, bo, heads):
            b, n, _ = x.shape
            j = ctx.shape[1]
            dh = wq.shape[1] // heads
            scale = dh ** (-0.5)
            q = (x @ wq).reshape(b, n, heads, dh).transpose(0, 2, 1, 3)
            k = (ctx @ wk).reshape(b, j, heads, dh).transpose(0, 2, 1, 3)
            v = (ctx @ wv).reshape(b, j, heads, dh).transpose(0, 2, 1, 3)
            sim = jnp.einsum('bhid,bhjd->bhij', q, k) * scale
            a = jax.nn.softmax(sim, axis=-1)
            out = jnp.einsum('bhij,bhjd->bhid', a, v)
            out = out.transpose(0, 2, 1, 3).reshape(b, n, heads * dh)
            return out @ wo + bo
        key = jax.random.key(seed)
        ks = jax.random.split(key, 24)
        r = lambda k, shp, s: jax.random.normal(k, shp, dtype=jnp.float32) * s
        d = {'x': r(ks[0], (8, 256, D), 1.0), 'context': r(ks[1], (8, 77, CTX), 1.0), 'heads': H, 'n1_g': jnp.ones((D,), jnp.float32), 'n1_b': jnp.zeros((D,), jnp.float32), 'q1': r(ks[2], (D, D), D ** (-0.5)), 'k1': r(ks[3], (D, D), D ** (-0.5)), 'v1': r(ks[4], (D, D), D ** (-0.5)), 'o1_w': r(ks[5], (D, D), D ** (-0.5)), 'o1_b': jnp.zeros((D,), jnp.float32), 'n2_g': jnp.ones((D,), jnp.float32), 'n2_b': jnp.zeros((D,), jnp.float32), 'q2': r(ks[6], (D, D), D ** (-0.5)), 'k2': r(ks[7], (CTX, D), CTX ** (-0.5)), 'v2': r(ks[8], (CTX, D), CTX ** (-0.5)), 'o2_w': r(ks[9], (D, D), D ** (-0.5)), 'o2_b': jnp.zeros((D,), jnp.float32), 'n3_g': jnp.ones((D,), jnp.float32), 'n3_b': jnp.zeros((D,), jnp.float32), 'ff_w1': r(ks[10], (D, 2 * FF_IN), D ** (-0.5)), 'ff_b1': jnp.zeros((2 * FF_IN,), jnp.float32), 'ff_w2': r(ks[11], (FF_IN, D), FF_IN ** (-0.5)), 'ff_b2': jnp.zeros((D,), jnp.float32)}
        return d
    _L1_xattn_all = _L1_xattn_setup()
    _L1_xattn_in = {k: v for k, v in _L1_xattn_all.items() if k in ('n1_g', 'n1_b', 'q1', 'k1', 'v1', 'o1_w', 'o1_b', 'n2_g', 'n2_b', 'q2', 'k2', 'v2', 'o2_w', 'o2_b', 'n3_g', 'n3_b', 'ff_w1', 'ff_b1', 'ff_w2', 'ff_b2')}
    del _L1_xattn_all
    return {'x': x, 'ctx_768': ctx_768, 'L0_xattn_n1_g': _L0_xattn_in['n1_g'], 'L0_xattn_n1_b': _L0_xattn_in['n1_b'], 'L0_xattn_q1': _L0_xattn_in['q1'], 'L0_xattn_k1': _L0_xattn_in['k1'], 'L0_xattn_v1': _L0_xattn_in['v1'], 'L0_xattn_o1_w': _L0_xattn_in['o1_w'], 'L0_xattn_o1_b': _L0_xattn_in['o1_b'], 'L0_xattn_n2_g': _L0_xattn_in['n2_g'], 'L0_xattn_n2_b': _L0_xattn_in['n2_b'], 'L0_xattn_q2': _L0_xattn_in['q2'], 'L0_xattn_k2': _L0_xattn_in['k2'], 'L0_xattn_v2': _L0_xattn_in['v2'], 'L0_xattn_o2_w': _L0_xattn_in['o2_w'], 'L0_xattn_o2_b': _L0_xattn_in['o2_b'], 'L0_xattn_n3_g': _L0_xattn_in['n3_g'], 'L0_xattn_n3_b': _L0_xattn_in['n3_b'], 'L0_xattn_ff_w1': _L0_xattn_in['ff_w1'], 'L0_xattn_ff_b1': _L0_xattn_in['ff_b1'], 'L0_xattn_ff_w2': _L0_xattn_in['ff_w2'], 'L0_xattn_ff_b2': _L0_xattn_in['ff_b2'], 'L1_xattn_n1_g': _L1_xattn_in['n1_g'], 'L1_xattn_n1_b': _L1_xattn_in['n1_b'], 'L1_xattn_q1': _L1_xattn_in['q1'], 'L1_xattn_k1': _L1_xattn_in['k1'], 'L1_xattn_v1': _L1_xattn_in['v1'], 'L1_xattn_o1_w': _L1_xattn_in['o1_w'], 'L1_xattn_o1_b': _L1_xattn_in['o1_b'], 'L1_xattn_n2_g': _L1_xattn_in['n2_g'], 'L1_xattn_n2_b': _L1_xattn_in['n2_b'], 'L1_xattn_q2': _L1_xattn_in['q2'], 'L1_xattn_k2': _L1_xattn_in['k2'], 'L1_xattn_v2': _L1_xattn_in['v2'], 'L1_xattn_o2_w': _L1_xattn_in['o2_w'], 'L1_xattn_o2_b': _L1_xattn_in['o2_b'], 'L1_xattn_n3_g': _L1_xattn_in['n3_g'], 'L1_xattn_n3_b': _L1_xattn_in['n3_b'], 'L1_xattn_ff_w1': _L1_xattn_in['ff_w1'], 'L1_xattn_ff_b1': _L1_xattn_in['ff_b1'], 'L1_xattn_ff_w2': _L1_xattn_in['ff_w2'], 'L1_xattn_ff_b2': _L1_xattn_in['ff_b2']}

def reference(x, ctx_768, L0_xattn_n1_g, L0_xattn_n1_b, L0_xattn_q1, L0_xattn_k1, L0_xattn_v1, L0_xattn_o1_w, L0_xattn_o1_b, L0_xattn_n2_g, L0_xattn_n2_b, L0_xattn_q2, L0_xattn_k2, L0_xattn_v2, L0_xattn_o2_w, L0_xattn_o2_b, L0_xattn_n3_g, L0_xattn_n3_b, L0_xattn_ff_w1, L0_xattn_ff_b1, L0_xattn_ff_w2, L0_xattn_ff_b2, L1_xattn_n1_g, L1_xattn_n1_b, L1_xattn_q1, L1_xattn_k1, L1_xattn_v1, L1_xattn_o1_w, L1_xattn_o1_b, L1_xattn_n2_g, L1_xattn_n2_b, L1_xattn_q2, L1_xattn_k2, L1_xattn_v2, L1_xattn_o2_w, L1_xattn_o2_b, L1_xattn_n3_g, L1_xattn_n3_b, L1_xattn_ff_w1, L1_xattn_ff_b1, L1_xattn_ff_w2, L1_xattn_ff_b2):
    import jax
    import jax.numpy as jnp

    def _L0_xattn_ref(x, context, heads, n1_g, n1_b, q1, k1, v1, o1_w, o1_b, n2_g, n2_b, q2, k2, v2, o2_w, o2_b, n3_g, n3_b, ff_w1, ff_b1, ff_w2, ff_b2):
        import jax, jax.numpy as jnp
        import numpy as np
        D = 320
        H = 20
        DH = D // H
        CTX = 192
        FF_IN = 4 * D
        EPS = 1e-05

        def _ln(x, g, b):
            m = jnp.mean(x, axis=-1, keepdims=True)
            v = jnp.mean(jnp.square(x - m), axis=-1, keepdims=True)
            return (x - m) * jax.lax.rsqrt(v + EPS) * g + b

        def _attn(x, ctx, wq, wk, wv, wo, bo, heads):
            b, n, _ = x.shape
            j = ctx.shape[1]
            dh = wq.shape[1] // heads
            scale = dh ** (-0.5)
            q = (x @ wq).reshape(b, n, heads, dh).transpose(0, 2, 1, 3)
            k = (ctx @ wk).reshape(b, j, heads, dh).transpose(0, 2, 1, 3)
            v = (ctx @ wv).reshape(b, j, heads, dh).transpose(0, 2, 1, 3)
            sim = jnp.einsum('bhid,bhjd->bhij', q, k) * scale
            a = jax.nn.softmax(sim, axis=-1)
            out = jnp.einsum('bhij,bhjd->bhid', a, v)
            out = out.transpose(0, 2, 1, 3).reshape(b, n, heads * dh)
            return out @ wo + bo
        h1 = _ln(x, n1_g, n1_b)
        x = _attn(h1, h1, q1, k1, v1, o1_w, o1_b, heads) + x
        h2 = _ln(x, n2_g, n2_b)
        x = _attn(h2, context, q2, k2, v2, o2_w, o2_b, heads) + x
        h3 = _ln(x, n3_g, n3_b)
        proj = h3 @ ff_w1 + ff_b1
        a, g = jnp.split(proj, 2, axis=-1)
        ff = a * jax.nn.gelu(g, approximate=False) @ ff_w2 + ff_b2
        return ff + x

    def _L1_xattn_ref(x, context, heads, n1_g, n1_b, q1, k1, v1, o1_w, o1_b, n2_g, n2_b, q2, k2, v2, o2_w, o2_b, n3_g, n3_b, ff_w1, ff_b1, ff_w2, ff_b2):
        import jax, jax.numpy as jnp
        import numpy as np
        D = 320
        H = 20
        DH = D // H
        CTX = 192
        FF_IN = 4 * D
        EPS = 1e-05

        def _ln(x, g, b):
            m = jnp.mean(x, axis=-1, keepdims=True)
            v = jnp.mean(jnp.square(x - m), axis=-1, keepdims=True)
            return (x - m) * jax.lax.rsqrt(v + EPS) * g + b

        def _attn(x, ctx, wq, wk, wv, wo, bo, heads):
            b, n, _ = x.shape
            j = ctx.shape[1]
            dh = wq.shape[1] // heads
            scale = dh ** (-0.5)
            q = (x @ wq).reshape(b, n, heads, dh).transpose(0, 2, 1, 3)
            k = (ctx @ wk).reshape(b, j, heads, dh).transpose(0, 2, 1, 3)
            v = (ctx @ wv).reshape(b, j, heads, dh).transpose(0, 2, 1, 3)
            sim = jnp.einsum('bhid,bhjd->bhij', q, k) * scale
            a = jax.nn.softmax(sim, axis=-1)
            out = jnp.einsum('bhij,bhjd->bhid', a, v)
            out = out.transpose(0, 2, 1, 3).reshape(b, n, heads * dh)
            return out @ wo + bo
        h1 = _ln(x, n1_g, n1_b)
        x = _attn(h1, h1, q1, k1, v1, o1_w, o1_b, heads) + x
        h2 = _ln(x, n2_g, n2_b)
        x = _attn(h2, context, q2, k2, v2, o2_w, o2_b, heads) + x
        h3 = _ln(x, n3_g, n3_b)
        proj = h3 @ ff_w1 + ff_b1
        a, g = jnp.split(proj, 2, axis=-1)
        ff = a * jax.nn.gelu(g, approximate=False) @ ff_w2 + ff_b2
        return ff + x
    x = _L0_xattn_ref(x, ctx_768, 20, L0_xattn_n1_g, L0_xattn_n1_b, L0_xattn_q1, L0_xattn_k1, L0_xattn_v1, L0_xattn_o1_w, L0_xattn_o1_b, L0_xattn_n2_g, L0_xattn_n2_b, L0_xattn_q2, L0_xattn_k2, L0_xattn_v2, L0_xattn_o2_w, L0_xattn_o2_b, L0_xattn_n3_g, L0_xattn_n3_b, L0_xattn_ff_w1, L0_xattn_ff_b1, L0_xattn_ff_w2, L0_xattn_ff_b2)
    x = _L1_xattn_ref(x, ctx_768, 20, L1_xattn_n1_g, L1_xattn_n1_b, L1_xattn_q1, L1_xattn_k1, L1_xattn_v1, L1_xattn_o1_w, L1_xattn_o1_b, L1_xattn_n2_g, L1_xattn_n2_b, L1_xattn_q2, L1_xattn_k2, L1_xattn_v2, L1_xattn_o2_w, L1_xattn_o2_b, L1_xattn_n3_g, L1_xattn_n3_b, L1_xattn_ff_w1, L1_xattn_ff_b1, L1_xattn_ff_w2, L1_xattn_ff_b2)
    return x

_drawn_inputs = setup_inputs


def setup_inputs(seed=0):
    import zlib

    import numpy as np

    out = dict(_drawn_inputs(seed))
    spreads = {'L0_xattn_n1_g': (1.0, 0.2),
     'L0_xattn_n1_b': (0.0, 0.1),
     'L0_xattn_o1_b': (0.0, 0.1),
     'L0_xattn_n2_g': (1.0, 0.2),
     'L0_xattn_n2_b': (0.0, 0.33),
     'L0_xattn_o2_b': (0.0, 0.1),
     'L0_xattn_n3_g': (1.0, 0.2),
     'L0_xattn_n3_b': (0.0, 0.1),
     'L0_xattn_ff_b1': (0.0, 0.1),
     'L0_xattn_ff_b2': (0.0, 0.1),
     'L1_xattn_n1_g': (1.0, 0.2),
     'L1_xattn_n1_b': (0.0, 0.1),
     'L1_xattn_o1_b': (0.0, 0.1),
     'L1_xattn_n2_g': (1.0, 0.6),
     'L1_xattn_n2_b': (0.0, 0.63),
     'L1_xattn_o2_b': (0.0, 0.1),
     'L1_xattn_n3_g': (1.0, 0.2),
     'L1_xattn_n3_b': (0.0, 0.1),
     'L1_xattn_ff_b1': (0.0, 0.1),
     'L1_xattn_ff_b2': (0.0, 0.1)}
    factors = {}
    for name, (base, spread) in spreads.items():
        noise = np.random.default_rng([zlib.crc32(name.encode()), seed]).standard_normal(out[name].shape)
        drawn = base * np.exp(spread * noise) if base else spread * noise
        out[name] = jnp.asarray(drawn.astype(out[name].dtype))
    for name, factor in factors.items():
        out[name] = (out[name] * factor).astype(out[name].dtype)
    return out
```

```python
from contextlib import ExitStack

import concourse.bass as bass
from concourse import mybir

F32 = mybir.dt.float32
F32R = mybir.dt.float32r
ALU = mybir.AluOpType
ACT = mybir.ActivationFunctionType
AX_X = mybir.AxisListType.X

P = 128
B, T, D = 4, 512, 320
L = 2
J, C = 1601, 192
H, DH = 20, 16
F = 4 * D
EPS = 1e-5
HG = 4
G = H // HG
TT = T // P
KC = 3
DC = [(c * P, min(P, D - c * P)) for c in range(KC)]
CC = C // 2
JP = J + 1
JT = (J + P - 1) // P
JN = [(n, min(512, JP - n)) for n in range(0, JP, 512)]
FM = F // P
RING = 3
DRING = 4
QK_RING = 3


class Attn:

    def __init__(self, keys, key_rows, units, unit_at, mt_at, stage, slot0, kt0, num0):
        self.keys = keys
        self.kt = len(key_rows)
        self.key_rows = key_rows
        self.units = units
        self.unit_at = unit_at
        self.mt_at = mt_at
        self.stage = stage
        self.slots = 4 * self.kt + 2
        self.slot0, self.kt0, self.num0 = slot0, kt0, num0

    def turn_slot(self, g):
        if isinstance(g, int) and g == 0:
            return self.slot0
        return g * self.slots + (self.slot0 + 1 - self.slots + 4 * (self.mt_at + 1))

    def bank_at(self, g):
        return g * (4 + 2 * len(self.units)) + (POS[self.stage] + 2 * len(self.units))


def spread(n, kt, first, last):
    at = [0] * kt
    for i in range(n):
        at[first + i * (last - first + 1) // n] += 1
    return at


HALF = 802
SELF_UNITS = [(h, (q, q + 1), 0, T) for h in range(HG) for q in range(0, TT, 2)]
CROSS_UNITS = [(h, (q,), n, min(HALF, JP - n)) for h in range(HG) for q in range(TT) for n in (0, HALF)]
SELF = Attn(T, [P] * TT, SELF_UNITS, [2, 3, 3, 0], 2, "max1", 0, 0, 0)
CROSS = Attn(JP, [min(P, J - k * P) for k in range(JT)], CROSS_UNITS, spread(len(CROSS_UNITS), JT, 1, 10), 11,
             "max2", G * SELF.slots, G * SELF.kt, G)
SLOTS = G * (SELF.slots + CROSS.slots)
KTS = G * (SELF.kt + CROSS.kt)
GROUPS = 2 * G
KT_CREDIT = 2 + TT
assert SELF.slots % RING == 0 and CROSS.slots % RING == 0 and SELF.kt0 % 2 == 0 and CROSS.kt0 % 2 == 0

STAGES = [("t1", KC, 1, 0), ("q1", KC, 1, 0), ("k1", KC, 1, 0), ("v1", TT, 1, 3),
          ("max1", G * len(SELF_UNITS) + 2 * (G + 1), 2, 0), ("o1", TT, 1, 0), ("t2", KC, 1, 0), ("q2", KC, 1, 0),
          ("tc", 2 * len(JN), 1, 0), ("k2", KC * len(JN), 1, 0), ("v2", JT, 1, 1),
          ("max2", G * len(CROSS_UNITS) + 2 * (G + 1), 2, 0), ("o2", TT, 1, 0), ("t3", KC, 1, 1), ("ff1", FM, 2, 0),
          ("ff2", TT, 1, 0)]
POS, COUNT, WIDTH, SKIP = {}, {}, {}, {}
BANKS = 0
for _name, _n, _w, _skip in STAGES:
    POS[_name], COUNT[_name], WIDTH[_name], SKIP[_name] = BANKS, _n, _w, _skip
    BANKS += _n * _w + _skip
assert BANKS % DRING == 0 and all(POS[s] % DRING == 0 for s in ("max1", "max2", "ff1"))


UNIT_PLACES = {0: (), 1: (3,), 2: (1, 4), 3: (0, 2, 4), 4: (0, 1, 3, 4)}


def done(stage, i=None):
    return POS[stage] + (COUNT[stage] if i is None else i + 1) * WIDTH[stage]


def begin(stage, i):
    return POS[stage] + (i + 1) * WIDTH[stage]


def step(stage, i):
    return WIDTH[stage] + (SKIP[stage] if i == COUNT[stage] - 1 else 0)


KEY_JOBS = [(c, n, cols) for n, cols in JN for c in range(KC)]
ROW_JOBS = [(c, 0, T) for c in range(KC)]
QK0 = {"q1": 0, "k1": KC, "q2": 2 * KC, "k2": 3 * KC}
QK_TILES = 3 * KC + len(KEY_JOBS)
assert QK_TILES % QK_RING == 0
STACK = {"q": (0, 1, 0), "k": (0, 0, 1)}
K_ROWS = 3 * DH
Q_ROWS = 64
STAGE_DMAS = 4
STORE_DMAS = 3
SMALL = ["q1", "k1", "v1", "q2"]


def blocks_kernel(nc, x, ctx_in, w, out):
    es = ExitStack()
    with es:
        def sb(name, shape, dt=F32):
            return es.enter_context(nc.sbuf_tensor(name, shape, dt))

        def sem(name):
            return es.enter_context(nc.semaphore(name))

        wsq = {n: sb("w_" + n, [P, KC, D]) for n in SMALL}
        wo = {n: sb("w_" + n, [P, G, D]) for n in ("o1", "o2")}
        wctx = {n: sb("w_" + n, [CC, 2, D]) for n in ("k2", "v2")}
        wff1 = sb("wff1", [P, 2, KC, 2, P])
        wff2 = sb("wff2", [P, FM, D])
        brow = sb("brow", [P, 3, D])
        gcol = sb("gcol", [P, 3, 2, KC])
        b1col = sb("b1col", [P, 2, FM])
        X = sb("X", [P, TT, D])
        XN = sb("XN", [P, TT, D])
        HN = sb("HN", [P, TT, D])
        hT = sb("hT", [P, KC, T])
        stats = sb("stats", [P, TT, 6])
        mv = sb("mv", [P, TT, 2])
        rstd = sb("rstd", [P, 2, TT])
        CT = sb("CT", [P, JT, C])
        cT_OA = sb("cT_OA", [P, 2 * JP])
        cT = cT_OA[0:CC, :].rearrange("p (c n) -> p c n", c=2)
        OA = cT_OA[:, 0:(G + 1) * T].rearrange("p (g n) -> p g n", g=G + 1)
        V_uT = sb("V_uT", [P, FM * T])
        V = V_uT[:, 0:JT * D].rearrange("p (k n) -> p k n", k=JT)
        uT = V_uT[:, :].rearrange("p (m n) -> p m n", m=FM)
        KS = sb("KS", [P, 2, 2, JP], F32R)
        QS = sb("QS", [P, 2, HG, T], F32R)
        VS = sb("VS", [P, 2, JT, HG, 32])
        ET = sb("ET", [P, 2, HG, T])
        QK = ET[:, :, :, :].rearrange("p a h n -> p (a h) n")
        OU = sb("OU", [P, T])
        RD = sb("RD", [P, TT, HG])
        mx = sb("mx", [P, TT, HG, 2])
        nm = sb("nm", [P, TT, HG])
        MS = sb("MS", [P, TT, 2, 2, 2])
        MT = sb("MT", [2 * HG, T])
        ident = sb("ident", [P, P])
        sel = sb("sel", [P, P])
        minus_half = sb("minus_half", [P, TT])

        pd = [es.enter_context(nc.psum_tensor(f"pd{i}", [P, 2, 512], F32)) for i in range(DRING // 2)]
        pr = [es.enter_context(nc.psum_tensor(f"pr{i}", [P, 512], F32)) for i in range(RING)]
        po = es.enter_context(nc.psum_tensor("po", [P, 512], F32))

        def bank(pos):
            return pd[(pos % DRING) // 2][:, pos % 2, :]

        def split_tile(q, part, rows, cols):
            return QK[0:rows, 2 * (q % QK_RING) + part, 0:cols]

        scr = {k: nc.dram_tensor("scr_" + k, (H, Q_ROWS if k[0] == "q" else K_ROWS, JP if k == "k2" else T), F32,
                                 kind="Internal").ap() for k in ("q1", "k1", "q2", "k2")}

        zeroed = sem("zeroed")
        consts = sem("consts")
        ones_in = sem("ones_in")
        x_copied = sem("x_copied")
        w_in = sem("w_in")
        x_in = sem("x_in")
        ctx_loaded = sem("ctx_loaded")
        wff1_in = [sem(f"wff1_in{i}") for i in range(2)]
        bank_ready = sem("bank_ready")
        bank_free = sem("bank_free")
        slot_ready = sem("slot_ready")
        slot_free = sem("slot_free")
        high_ready = sem("high_ready")
        stored = [sem(f"stored{i}") for i in range(QK_RING)]
        stats_done = sem("stats_done")
        mean_done = sem("mean_done")
        var_done = sem("var_done")
        rstd_done = sem("rstd_done")
        norm_done = sem("norm_done")
        bias_done = sem("bias_done")
        staged = sem("staged")
        vals_staged = sem("vals_staged")
        keys_done = sem("keys_done")
        sums_out = sem("sums_out")
        max_steps = sem("max_steps")
        max_in = sem("max_in")
        gate_done = sem("gate_done")
        x_stored = sem("x_stored")
        passed = sem("passed")

        block = es.enter_context(nc.Block())

        def alone(eng):
            eng.sem_inc(passed, 1)

        def pairs(eng, group):
            with eng.Fori(0, G // 2) as i:
                group(i * 2, 0)
                group(i * 2 + 1, 1)
            group(G - 1, 0)

        W_LOADS = 4 * KC + 2 * HG + 2 + 3 + 6 * KC + 2

        cleared = [t[:, :, :] for t in (*wsq.values(), *wo.values(), hT)]
        cleared += [wff1[:, :, :, :, :], VS[:, :, :, :, :], QS[:, :, :, :].bitcast(F32), KS[:, :, :, :].bitcast(F32),
                    V_uT[:, :], ident[:, :], sel[:, :]]
        CONSTS = 6

        @block.sync
        def _(sp):
            sp.dma_start(out.rearrange("b (s p) d -> (b s) (p d)", p=32),
                         x.rearrange("b (s p) d -> (b s) (p d)", p=32)).then_inc(x_copied, 16)
            for s in stored:
                sp.sem_inc(s, 16 * STORE_DMAS)
            sp.sem_inc(max_in, 32)
            sp.sem_inc(x_stored, 16)
            sp.wait_ge(x_copied, 16)
            sp.wait_ge(consts, CONSTS)
            ones = CT[0:2, :, :].rearrange("p t c -> p (t c)")[:, 0:JP]
            for par in range(2):
                for pair in range(2):
                    for e in (0, 64):
                        sp.dma_start(KS[e + 3 * DH:e + 3 * DH + 2, par, pair, :].bitcast(F32), ones
                                     ).then_inc(ones_in, 16)
            sp.wait_ge(zeroed, len(cleared))
            for k in ("q1", "q2"):
                for h in (0, H // 2):
                    sp.dma_start(scr[k][h:h + H // 2, K_ROWS:Q_ROWS, :].rearrange("h r n -> r h n"),
                                 V_uT[0:Q_ROWS - K_ROWS, :].rearrange("p (h n) -> p h n", h=H // 2)
                                 ).then_inc(ones_in, 16)
            sp.wait_ge(ones_in, 16 * 12)

            def load_entry(b):
                full = (JT - 1) * P
                sp.dma_start(XN[:, :, :], out[bass.ds(b, 1)].rearrange("b (t p) d -> p (b t) d", p=P)
                             ).then_inc(x_in, 16)
                sp.dma_start(CT[:, 0:JT - 1, :], ctx_in[bass.ds(b, 1), 0:full, :].rearrange(
                    "b (t p) c -> p (b t) c", p=P)).then_inc(ctx_loaded, 16)
                sp.dma_start(CT[0:J - full, JT - 1, :], ctx_in[bass.ds(b, 1), full:J, :].rearrange(
                    "b p c -> (b p) c")).then_inc(ctx_loaded, 16)

            load_entry(0)
            with sp.Fori(0, L) as l:
                def load(dst, src):
                    sp.dma_start(dst, src).then_inc(w_in, 16)

                def layer(name):
                    a = w[name]
                    return a[bass.ds(l, 1)].rearrange(
                        "l " + " ".join("abc"[:len(a.shape) - 1]) + " -> (l a) " + " ".join("bc"[:len(a.shape) - 2]))

                for i in range(3):
                    for j, k in enumerate("gb"):
                        for c, (r, m) in enumerate(DC):
                            load(gcol[0:m, i, j, c:c + 1], layer(f"n{i + 1}_{k}")[r:r + m].rearrange(
                                "(p a) -> p a", a=1))
                for k in SMALL:
                    for c, (r, m) in enumerate(DC):
                        load(wsq[k][0:m, c, :], layer(k)[r:r + m, :])
                for i, k in enumerate(("o1_b", "o2_b", "ff_b2")):
                    load(brow[:, i, :], w[k][bass.ds(l, 1), :].partition_broadcast(P))
                for k in ("o1", "o2"):
                    src = layer(k + "_w").rearrange("(g h d) n -> h d g n", h=HG, d=DH)
                    for h in range(HG):
                        load(wo[k][32 * h:32 * h + DH, :, :], src[h])
                for k in ("k2", "v2"):
                    load(wctx[k][:, :, :], layer(k).rearrange("(c p) n -> p c n", c=2))
                load(b1col[:, :, :], w["ff_b1"][bass.ds(l, 1)].rearrange("l p a m -> (l p) a m"))
                load(wff2[:, :, :], layer("ff_w2").rearrange("(m p) n -> p m n", p=P))
                with sp.Fori(0, B) as b:
                    it = l * B + b
                    entry = out[bass.ds(b, 1)].rearrange("b (t p) d -> p (b t) d", p=P)
                    def store(kind, jobs):
                        for i, (c, n0, cols) in enumerate(jobs):
                            q, (r, m) = QK0[kind] + i, DC[c]
                            sp.wait_ge(bank_free, it * BANKS + DRING + done(kind, i))
                            for k, part in enumerate(STACK[kind[0]]):
                                sp.dma_start(scr[kind][r // DH:(r + m) // DH, k * DH:(k + 1) * DH, n0:n0 + cols],
                                             split_tile(q, part, m, cols)).then_inc(stored[q % QK_RING], 16)

                    def wait_stored(tiles):
                        for s in range(QK_RING):
                            n = (tiles - s + QK_RING - 1) // QK_RING
                            sp.wait_ge(stored[s], it * (16 * STORE_DMAS * QK_TILES // QK_RING) + 16 * STORE_DMAS * (1 + n))
                            alone(sp)

                    def attention(a, qs, ks):
                        def group(g, par):
                            if not (isinstance(g, int) and g == 0):
                                sp.wait_ge(slot_ready, it * SLOTS + g * a.slots + (a.slot0 - a.slots + 1))
                            for e in range(2):
                                sp.dma_start(KS[64 * e:64 * e + K_ROWS, par, :, 0:a.keys].bitcast(F32),
                                             ks[bass.ds(g * HG + e, HG // 2, 2), :, :].rearrange("h r n -> r h n")
                                             ).then_inc(staged, 16)
                                sp.dma_start(QS[64 * e:64 * e + Q_ROWS, par, e::2, :].bitcast(F32),
                                             qs[bass.ds(g * HG + e, HG // 2, 2), :, :].rearrange("h r n -> r h n")
                                             ).then_inc(staged, 16)
                            sp.wait_ge(slot_free, it * SLOTS + RING + 1 + a.turn_slot(g))
                            for e in range(2):
                                r = 64 * e + K_ROWS
                                sp.dma_start(QS[r:r + 2, par, e::2, :].bitcast(F32), MT[4 * e:4 * e + 4, :]
                                             ).then_inc(max_in, 16)
                        group(0, 0)
                        with sp.Fori(0, G // 2) as i:
                            group(i * 2 + 1, 1)
                            group(i * 2 + 2, 0)

                    store("q1", ROW_JOBS)
                    store("k1", ROW_JOBS)
                    wait_stored(QK0["q2"])
                    attention(SELF, scr["q1"], scr["k1"])
                    store("q2", ROW_JOBS)
                    store("k2", KEY_JOBS)
                    wait_stored(QK_TILES)
                    sp.wait_ge(bias_done, it * (3 * TT) + TT)
                    alone(sp)
                    sp.wait_ge(bank_free, it * BANKS + DRING + done("tc"))
                    alone(sp)
                    load_entry((b + 1) % B)
                    attention(CROSS, scr["q2"], scr["k2"])
                    with sp.Fori(0, FM // 2) as i:
                        for a in range(2):
                            m = i * 2 + a
                            sp.wait_ge(bank_ready, it * BANKS + m * 2 + (POS["ff1"] - 2))
                            for v in range(2):
                                for c, (r, rows) in enumerate(DC):
                                    sp.dma_start(wff1[0:rows, a, c, v, :],
                                                 w["ff_w1"][bass.ds(l, 1), r:r + rows, bass.ds(m * P + v * F, P)
                                                            ].rearrange("l p n -> (l p) n")).then_inc(wff1_in[a], 16)
                    sp.wait_ge(bank_free, it * BANKS + DRING + BANKS)
                    sp.dma_start(entry, X[:, :, :]).then_inc(x_stored, 16)
                    sp.wait_ge(x_stored, it * 16 + 32)
                    alone(sp)
            sp.wait_ge(x_in, 16 * (L * B + 1))
            sp.wait_ge(ctx_loaded, 32 * (L * B + 1))

        @block.gpsimd
        def _(pool):
            gp = nc.gpsimd
            for t in cleared:
                gp.memset(t, 0.0).then_inc(zeroed, 1)
            pool.sem_inc(vals_staged, 1)
            gp.memset(minus_half[:, :], -0.5).then_inc(consts, 1)
            gp.memset(OU[:, :], 1.0).then_inc(consts, 1)
            gp.memset(CT[:, :, :], 1.0).then_inc(consts, 1)
            pool.wait_ge(zeroed, len(cleared))
            gp.affine_select(out=ident[:, :], in_=ident[:, :], compare_op=ALU.not_equal, fill=1.0,
                             base=0, pattern=[[-1, P]], channel_multiplier=1).then_inc(consts, 1)
            of_head = sel[:, :].rearrange("p (a m) -> p a m", a=HG)
            gp.affine_select(out=of_head, in_=of_head, compare_op=ALU.not_equal, fill=1.0,
                             base=-DH, pattern=[[-32, HG], [0, 32]], channel_multiplier=1).then_inc(consts, 1)
            gp.memset(VS[:, :, :, :, DH:DH + 1], 1.0).then_inc(consts, 1)
            with pool.Fori(0, L) as l:
                pool.wait_ge(w_in, l * (16 * W_LOADS) + 16 * W_LOADS)
                alone(pool)
                with pool.Fori(0, B) as b:
                    it = l * B + b

                    def norm_scale(i):
                        pool.wait_ge(mean_done, it * (3 * TT) + TT * (i + 1))
                        alone(pool)
                        gp.tensor_scalar(rstd[:, 0, :], mv[:, :, 1], EPS, None, ALU.add).then_inc(var_done, 1)
                        pool.wait_ge(var_done, it * 3 + i + 1)
                        gp.tensor_tensor(rstd[:, 1, :], rstd[:, 0, :], minus_half[:, :], ALU.pow
                                         ).then_inc(rstd_done, 1)
                        pool.wait_ge(norm_done, it * (3 * TT) + TT * (i + 1))
                        if i == 0:
                            pool.wait_ge(x_stored, it * 16 + 16)
                        for t in range(TT):
                            gp.tensor_tensor(X[:, t, :], (X if i else XN)[:, t, :], brow[:, i, :], ALU.add
                                             ).then_inc(bias_done, 1)

                    def attention(a, stage):
                        def stage_values(g, par):
                            pool.wait_ge(keys_done, it * KTS + g * a.kt + (KT_CREDIT + a.kt0 - a.kt))
                            alone(pool)
                            for k in range(0, a.kt, 4):
                                n = min(4, a.kt - k)
                                ins = gp.tensor_copy(VS[:, par, k:k + n, :, 0:DH],
                                                     V[:, k:k + n, bass.ds(g * (HG * DH), HG * DH)].rearrange(
                                                         "p k (h d) -> p k h d", h=HG))
                            ins.then_inc(vals_staged, 1)

                        pool.wait_ge(bank_free, it * BANKS + DRING + done(stage))
                        alone(pool)
                        pairs(pool, stage_values)

                    norm_scale(0)
                    attention(SELF, "v1")
                    norm_scale(1)
                    attention(CROSS, "v2")
                    norm_scale(2)

        @block.scalar
        def _(act):
            act.sem_inc(slot_free, RING)
            act.sem_inc(sums_out, 1)
            with act.Fori(0, L) as l:
                act.wait_ge(w_in, l * (16 * W_LOADS) + 16 * W_LOADS)
                with act.Fori(0, B) as b:
                    it = l * B + b

                    def high(kind, jobs, scale):
                        for i, (c, n0, cols) in enumerate(jobs):
                            q, m = QK0[kind] + i, DC[c][1]
                            act.wait_ge(bank_ready, it * BANKS + done(kind, i))
                            act.wait_ge(stored[q % QK_RING], it * (16 * STORE_DMAS * QK_TILES // QK_RING) + 16 * STORE_DMAS * (1 + q // QK_RING))
                            nc.scalar.activation(split_tile(q, 0, m, cols).bitcast(F32R),
                                                 bank(POS[kind] + i)[0:m, 0:cols], ACT.Copy, scale=scale
                                                 ).then_inc(high_ready, 1)

                    def attention(a):
                        def turn(g, r, slot):
                            act.wait_ge(max_in, it * (32 * GROUPS) + g * 32 + 32 * (a.num0 + 1))
                            act.wait_ge(slot_ready, it * SLOTS + slot + 2)
                            nc.scalar.copy(MT[:, :], pr[r % RING][0:2 * HG, :]).then_inc(slot_free, 1)

                        def group(g, par, last=False):
                            r, slot = 1, g * a.slots + (a.slot0 + 1)
                            for k, m in enumerate(a.key_rows):
                                act.wait_ge(keys_done, it * KTS + g * a.kt + (a.kt0 + k + KT_CREDIT - 1))
                                for h in range(HG):
                                    act.wait_ge(slot_ready, it * SLOTS + slot + 2)
                                    skip = k == a.kt - 1 and h == HG - 1
                                    nc.scalar.activation(ET[0:m, (par * a.kt + k) % 2, h, :], pr[r % RING][0:m, :],
                                                         ACT.Exp).then_inc(slot_free, 2 if skip else 1)
                                    r, slot = r + 1, slot + 1
                                if k == a.mt_at and not last:
                                    turn(g + 1, r, slot)
                                    r, slot = r + 1, slot + 1
                            act.wait_ge(keys_done, it * KTS + g * a.kt + (a.kt0 + a.kt + KT_CREDIT))
                            act.wait_ge(bank_free, it * BANKS + (a.bank_at(g) + 4 + DRING))
                            nc.scalar.copy(OU[:, :], po[:, :]).then_inc(sums_out, 1)

                        turn(0, 0, a.slot0)
                        with act.Fori(0, G // 2) as i:
                            group(i * 2, 0)
                            group(i * 2 + 1, 1)
                        group(G - 1, 0, last=True)

                    high("q1", ROW_JOBS, DH ** -0.5)
                    high("k1", ROW_JOBS, 1.0)
                    attention(SELF)
                    high("q2", ROW_JOBS, DH ** -0.5)
                    high("k2", KEY_JOBS, 1.0)
                    attention(CROSS)
                    with act.Fori(0, FM // 2) as i:
                        for j in range(2):
                            m = i * 2 + j
                            act.wait_ge(bank_ready, it * BANKS + m * 2 + (POS["ff1"] + 1))
                            act.wait_ge(bank_free, it * BANKS + m * 2 + (POS["ff1"] + DRING - 2))
                            nc.scalar.activation(ET[:, 0, j, :], bank(2 * j), ACT.Gelu,
                                                 bias=b1col[:, 1, bass.ds(m, 1)]).then_inc(gate_done, 1)

        @block.vector
        def _(dve):
            v = nc.vector
            dve.sem_inc(bank_free, DRING)
            with dve.Fori(0, L) as l:
                dve.wait_ge(w_in, l * (16 * W_LOADS) + 16 * W_LOADS)
                alone(dve)
                with dve.Fori(0, B) as b:
                    it = l * B + b

                    def normalise(i):
                        src = X if i else XN
                        for t in range(TT):
                            v.bn_stats(stats[:, t, :], src[:, t, :]).then_inc(stats_done, 1)
                        for t in range(TT):
                            dve.wait_ge(stats_done, it * (3 * TT) + TT * i + t + 1)
                            alone(dve)
                            v.bn_aggr(mv[:, t, :], stats[:, t, :]).then_inc(mean_done, 1)
                        dve.wait_ge(rstd_done, it * 3 + i + 1)
                        for t in range(TT):
                            v.tensor_scalar(HN[:, t, :], src[:, t, :], mv[:, t, 0:1], rstd[:, 1, t:t + 1],
                                            ALU.subtract, ALU.mult).then_inc(norm_done, 1)
                        stage = f"t{i + 1}"
                        for c, (r, m) in enumerate(DC):
                            dve.wait_ge(bank_ready, it * BANKS + done(stage, c))
                            v.tensor_scalar(hT[0:m, c, :], bank(POS[stage] + c)[0:m, :], gcol[0:m, i, 0, c:c + 1],
                                            gcol[0:m, i, 1, c:c + 1], ALU.mult, ALU.add
                                            ).then_inc(bank_free, step(stage, c))

                    def low(kind, jobs, scale):
                        for i, (c, n0, cols) in enumerate(jobs):
                            q, m = QK0[kind] + i, DC[c][1]
                            dve.wait_ge(high_ready, it * QK_TILES + q + 1)
                            v.scalar_tensor_tensor(split_tile(q, 1, m, cols), bank(POS[kind] + i)[0:m, 0:cols],
                                                   scale, split_tile(q, 0, m, cols), ALU.mult, ALU.subtract
                                                   ).then_inc(bank_free, step(kind, i))

                    def take_values(stage, rows, groups):
                        dve.wait_ge(vals_staged, it * GROUPS + groups + 1)
                        for k, m in enumerate(rows):
                            dve.wait_ge(bank_ready, it * BANKS + done(stage, k))
                            v.tensor_copy(V[0:m, k, :], bank(POS[stage] + k)[0:m, 0:D]
                                          ).then_inc(bank_free, step(stage, k))

                    def attention(a):
                        def maxima(g, at):
                            for u, (h, qts, n0, cols) in enumerate(a.units):
                                dve.wait_ge(bank_ready, it * BANKS + at + (2 * u + 2))
                                both = pd[u % 2]
                                if a is SELF:
                                    v.reduce_max(mx[:, qts[0]:qts[0] + 2, h, 0], both[:, :, 0:cols], AX_X
                                                 ).then_inc(bank_free, 2)
                                else:
                                    v.reduce_max(mx[:, qts[0], h, n0 // HALF:n0 // HALF + 1],
                                                 both[:, :, :].rearrange("p a n -> p (a n)")[:, 0:cols], AX_X
                                                 ).then_inc(bank_free, 2)
                            dve.wait_ge(bank_free, it * BANKS + at + (2 * len(a.units) + DRING))
                            by_parity = nm[:, :, :].rearrange("p t (b e) -> p t e b", e=2)
                            v.tensor_reduce(nm[:, :, :], mx[:, :, :, 0:1 if a is SELF else 2], AX_X, ALU.max,
                                            negate=True).then_inc(max_steps, 1)
                            dve.wait_ge(max_steps, it * (3 * GROUPS) + g * 3 + (3 * a.num0 + 1))
                            v.tensor_copy(MS[:, :, :, 0, :].bitcast(F32R), by_parity).then_inc(max_steps, 1)
                            dve.wait_ge(max_steps, it * (3 * GROUPS) + g * 3 + (3 * a.num0 + 2))
                            v.tensor_tensor(MS[:, :, :, 1, :], by_parity, MS[:, :, :, 0, :], ALU.subtract
                                            ).then_inc(max_steps, 1)

                        def divide(g, at):
                            dve.wait_ge(bank_ready, it * BANKS + at + 2)
                            v.reciprocal(RD[:, :, :].rearrange("p t h -> p (t h)"), pd[0][:, 0, 0:TT * HG]
                                         ).then_inc(bank_free, 2)
                            dve.wait_ge(bank_ready, it * BANKS + at + 4)
                            dst = OA[:, G, :] if g is G else OA[:, bass.ds(g, 1), :].rearrange("p g n -> p (g n)")
                            v.tensor_tensor(dst, pd[1][:, 0, :], OU[:, :], ALU.mult).then_inc(bank_free, 2)

                        maxima(0, POS[a.stage])
                        with dve.Fori(0, G - 1) as i:
                            divide(i, a.bank_at(i))
                            maxima(i + 1, a.bank_at(i) + 4)
                        divide(G - 1, a.bank_at(G - 1))
                        divide(G, a.bank_at(G - 1) + 4)

                    def add_to_x(stage, biases):
                        for t in range(TT):
                            dve.wait_ge(bias_done, it * (3 * TT) + TT * biases + t + 1)
                            dve.wait_ge(bank_ready, it * BANKS + done(stage, t))
                            v.tensor_tensor(X[:, t, :], bank(POS[stage] + t)[:, 0:D], X[:, t, :], ALU.add
                                            ).then_inc(bank_free, step(stage, t))
                        dve.wait_ge(bank_free, it * BANKS + DRING + done(stage))
                        alone(dve)

                    dve.wait_ge(x_in, it * 16 + 16)
                    normalise(0)
                    low("q1", ROW_JOBS, DH ** -0.5)
                    low("k1", ROW_JOBS, 1.0)
                    take_values("v1", SELF.key_rows, 0)
                    attention(SELF)
                    add_to_x("o1", 0)
                    normalise(1)
                    low("q2", ROW_JOBS, DH ** -0.5)
                    for c in range(2):
                        for i, (n0, cols) in enumerate(JN):
                            j = c * len(JN) + i
                            dve.wait_ge(bank_ready, it * BANKS + done("tc", j))
                            if n0 + cols > J:
                                v.tensor_copy(cT[:, c, J:JP], bank(POS["tc"] + j)[0:CC, J - 1 - n0:J - n0])
                                cols = J - n0
                            v.tensor_copy(cT[:, c, n0:n0 + cols], bank(POS["tc"] + j)[0:CC, 0:cols]
                                          ).then_inc(bank_free, step("tc", j))
                    low("k2", KEY_JOBS, 1.0)
                    take_values("v2", CROSS.key_rows, G)
                    attention(CROSS)
                    add_to_x("o2", 1)
                    normalise(2)
                    with dve.Fori(0, FM // 2) as i:
                        for j in range(2):
                            m = i * 2 + j
                            dve.wait_ge(bank_ready, it * BANKS + m * 2 + (POS["ff1"] + 2))
                            dve.wait_ge(gate_done, it * FM + m + 1)
                            v.scalar_tensor_tensor(uT[:, bass.ds(m, 1), :].rearrange("p m n -> p (m n)"),
                                                   bank(2 * j + 1), b1col[:, 0, bass.ds(m, 1)], ET[:, 0, j, :],
                                                   ALU.add, ALU.mult).then_inc(bank_free, 2)
                    add_to_x("ff2", 2)

        @block.tensor
        def _(pe):
            mm = nc.tensor.matmul
            pe.sem_inc(keys_done, KT_CREDIT)
            pe.sem_inc(slot_ready, 1)
            pe.wait_ge(zeroed, len(cleared))
            pe.wait_ge(consts, CONSTS)
            pe.wait_ge(ones_in, 16 * 12)
            with pe.Fori(0, L) as l:
                pe.wait_ge(w_in, l * (16 * W_LOADS) + 16 * W_LOADS)
                alone(pe)
                with pe.Fori(0, B) as b:
                    it = l * B + b

                    def turn_norm(i):
                        stage = f"t{i + 1}"
                        for c, (r, m) in enumerate(DC):
                            pe.wait_ge(bank_free, it * BANKS + begin(stage, c))
                            alone(pe)
                            for t in range(TT):
                                if c == 0:
                                    pe.wait_ge(norm_done, it * (3 * TT) + TT * i + t + 1)
                                ins = nc.tensor.transpose(bank(POS[stage] + c)[0:m, t * P:(t + 1) * P],
                                                          HN[:, t, r:r + m], ident[:, :])
                            ins.then_inc(bank_ready, step(stage, c))

                    def project(kind):
                        for c, (r, m) in enumerate(DC):
                            pe.wait_ge(bank_free, it * BANKS + begin(kind, c))
                            for k in range(KC):
                                ins = mm(bank(POS[kind] + c)[0:m, :], wsq[kind][:, k, r:r + m], hT[:, k, :],
                                         start=k == 0, stop=k == KC - 1)
                            ins.then_inc(bank_ready, step(kind, c))

                    def attention(a):
                        def unit(par, u, at):
                            h, qts, n0, cols = a.units[u]
                            pe.wait_ge(bank_free, it * BANKS + at + (2 * u + 2))
                            if a is SELF:
                                parts = [(q, j, 0, cols) for j, q in enumerate(qts)]
                            else:
                                parts = [(qts[0], 0, n0, 512), (qts[0], 1, n0 + 512, cols - 512)]
                            for q, j, n, width in parts:
                                ins = mm(pd[u % 2][:, j, 0:width], QS[:, par, h, q * P:(q + 1) * P],
                                         KS[:, par, h // 2, n:n + width], start=True, stop=True)
                            ins.then_inc(bank_ready, 2)

                        def turn_max(g, r, slot):
                            pe.wait_ge(slot_free, it * SLOTS + slot + 1)
                            pe.wait_ge(max_steps, it * (3 * GROUPS) + g * 3 + 3 * (a.num0 + 1))
                            for q in range(TT):
                                ins = mm(pr[r % RING][0:2 * HG, q * P:(q + 1) * P],
                                         MS[:, q, :, :, :].rearrange("p e a b -> p (e a b)"), ident[:, :],
                                         start=True, stop=True)
                            ins.then_inc(slot_ready, 1)

                        def weigh(g, par, k, last):
                            m = a.key_rows[k]
                            for h in range(HG):
                                n = 4 * (k + 1) + (1 if k > a.mt_at and not last else 0)
                                if h == 0:
                                    pe.wait_ge(slot_free, it * SLOTS + g * a.slots + (a.slot0 + 1 + n + RING))
                                ins = mm(po[32 * h:32 * h + 32, :], VS[0:m, par, k, h, :],
                                         ET[0:m, (par * a.kt + k) % 2, h, :], start=k == 0, stop=k == a.kt - 1)
                            ins.then_inc(keys_done, 1)

                        def turn_divisors(g, at):
                            pe.wait_ge(sums_out, it * GROUPS + g + (a.num0 + 1))
                            pe.wait_ge(bank_free, it * BANKS + at + 2)
                            for q in range(TT):
                                ins = mm(pd[0][:, 0, q * HG:(q + 1) * HG], OU[:, q * P:(q + 1) * P], sel[:, ::32],
                                         start=True, stop=True)
                            ins.then_inc(bank_ready, 2)

                        def spread_reciprocals(at):
                            pe.wait_ge(bank_free, it * BANKS + at + (DRING + 2))
                            for q in range(TT):
                                for h in range(HG):
                                    ins = mm(pd[1][32 * h:32 * h + 32, 0, q * P:(q + 1) * P],
                                             RD[:, q, h:h + 1].to_broadcast([P, 32]), ident[:, :],
                                             start=True, stop=True)
                            ins.then_inc(bank_ready, 2)

                        def group(g, par, last=False):
                            r, slot, u = 1, g * a.slots + (a.slot0 + 1), 0
                            at = a.bank_at(g)
                            nxt = g + 1

                            def next_unit(k, place, u):
                                places = (3, 4) if k == 0 else UNIT_PLACES[a.unit_at[k]]
                                if last or place not in places[:a.unit_at[k]]:
                                    return u
                                if u == 0:
                                    pe.wait_ge(staged, it * (16 * STAGE_DMAS * GROUPS) + nxt * (16 * STAGE_DMAS)
                                               + 16 * STAGE_DMAS * (a.num0 + 1))
                                unit(1 - par, u, at + 4)
                                return u + 1

                            pe.wait_ge(max_in, it * (32 * GROUPS) + g * 32 + 32 * (a.num0 + 2))
                            for k, m in enumerate(a.key_rows):
                                for h in range(HG):
                                    pe.wait_ge(slot_free, it * SLOTS + slot + 1)
                                    skip = k == a.kt - 1 and h == HG - 1
                                    mm(pr[r % RING][0:m, :], KS[:, par, h // 2, k * P:k * P + m], QS[:, par, h, :],
                                       start=True, stop=True).then_inc(slot_ready, 2 if skip else 1)
                                    r, slot = r + 1, slot + 1
                                    if k == 0 and h == 2:
                                        turn_divisors(g, at)
                                    if k == 0 and h == 3:
                                        spread_reciprocals(at)
                                    u = next_unit(k, h, u)
                                if k == 1:
                                    pe.wait_ge(vals_staged, it * GROUPS + g + (a.num0 + 2))
                                if k:
                                    weigh(g, par, k - 1, last)
                                u = next_unit(k, 4, u)
                                if k == a.mt_at and not last:
                                    turn_max(nxt, r, slot)
                                    r, slot = r + 1, slot + 1
                            weigh(g, par, a.kt - 1, last)
                            if last:
                                turn_divisors(G, at + 4)
                                spread_reciprocals(at + 4)

                        pe.wait_ge(staged, it * (16 * STAGE_DMAS * GROUPS) + 16 * STAGE_DMAS * (a.num0 + 1))
                        for u in range(len(a.units)):
                            unit(0, u, POS[a.stage])
                        turn_max(0, 0, a.slot0)
                        with pe.Fori(0, G // 2) as i:
                            group(i * 2, 0)
                            group(i * 2 + 1, 1)
                        group(G - 1, 0, last=True)

                    def project_out(kind):
                        pe.wait_ge(bank_free, it * BANKS + (DRING + POS[kind]))
                        for t in range(TT):
                            pe.wait_ge(bank_free, it * BANKS + begin(kind, t))
                            for g in range(G):
                                ins = mm(bank(POS[kind] + t)[:, 0:D], OA[:, g + 1, t * P:(t + 1) * P], wo[kind][:, g, :],
                                         start=g == 0, stop=g == G - 1)
                            ins.then_inc(bank_ready, step(kind, t))

                    turn_norm(0)
                    pe.wait_ge(bank_free, it * BANKS + (DRING + done("t1")))
                    project("q1")
                    project("k1")
                    for t in range(TT):
                        pe.wait_ge(bank_free, it * BANKS + begin("v1", t))
                        for k in range(KC):
                            ins = mm(bank(POS["v1"] + t)[:, 0:D], hT[:, k, t * P:(t + 1) * P], wsq["v1"][:, k, :],
                                     start=k == 0, stop=k == KC - 1)
                        ins.then_inc(bank_ready, step("v1", t))
                    attention(SELF)
                    project_out("o1")
                    turn_norm(1)
                    pe.wait_ge(bank_free, it * BANKS + (DRING + done("t2")))
                    project("q2")
                    pe.wait_ge(ctx_loaded, it * 32 + 32)
                    for c in range(2):
                        for i, (n0, cols) in enumerate(JN):
                            j = c * len(JN) + i
                            pe.wait_ge(bank_free, it * BANKS + begin("tc", j))
                            for k in range(n0 // P, min(JT, n0 // P + 4)):
                                m = CROSS.key_rows[k]
                                ins = nc.tensor.transpose(bank(POS["tc"] + j)[0:CC, k * P - n0:k * P - n0 + m],
                                                          CT[0:m, k, c * CC:(c + 1) * CC], ident[0:m, 0:m])
                            ins.then_inc(bank_ready, step("tc", j))
                    pe.wait_ge(bank_free, it * BANKS + (DRING + done("tc")))
                    for j, (c, n0, cols) in enumerate(KEY_JOBS):
                        r, m = DC[c]
                        pe.wait_ge(bank_free, it * BANKS + begin("k2", j))
                        for k in range(2):
                            ins = mm(bank(POS["k2"] + j)[0:m, 0:cols], wctx["k2"][:, k, r:r + m],
                                     cT[:, k, n0:n0 + cols], start=k == 0, stop=k == 1)
                        ins.then_inc(bank_ready, step("k2", j))
                    for j, m in enumerate(CROSS.key_rows):
                        pe.wait_ge(bank_free, it * BANKS + begin("v2", j))
                        for k in range(2):
                            ins = mm(bank(POS["v2"] + j)[0:m, 0:D], cT[:, k, j * P:j * P + m], wctx["v2"][:, k, :],
                                     start=k == 0, stop=k == 1)
                        ins.then_inc(bank_ready, step("v2", j))
                    attention(CROSS)
                    project_out("o2")
                    turn_norm(2)
                    pe.wait_ge(bank_free, it * BANKS + (DRING + done("t3")))
                    alone(pe)
                    with pe.Fori(0, FM // 2) as i:
                        for j in range(2):
                            m = i * 2 + j
                            pe.wait_ge(wff1_in[j], it * (16 * 2 * KC * (FM // 2)) + i * (16 * 2 * KC) + 16 * 2 * KC)
                            pe.wait_ge(bank_free, it * BANKS + m * 2 + (POS["ff1"] + 2))
                            for side in (1, 0):
                                for k in range(KC):
                                    ins = mm(bank(2 * j + 1 - side), wff1[:, j, k, side, :], hT[:, k, :],
                                             start=k == 0, stop=k == KC - 1)
                                ins.then_inc(bank_ready, 1)
                    pe.wait_ge(bank_free, it * BANKS + (DRING + done("ff1")))
                    for t in range(TT):
                        pe.wait_ge(bank_free, it * BANKS + begin("ff2", t))
                        for m in range(FM):
                            ins = mm(bank(POS["ff2"] + t)[:, 0:D], uT[:, m, t * P:(t + 1) * P], wff2[:, m, :],
                                     start=m == 0, stop=m == FM - 1)
                        ins.then_inc(bank_ready, step("ff2", t))


_W = ["n1_g", "n1_b", "q1", "k1", "v1", "o1_w", "o1_b", "n2_g", "n2_b", "q2", "k2", "v2", "o2_w", "o2_b",
      "n3_g", "n3_b", "ff_w1", "ff_b1", "ff_w2", "ff_b2"]


def kernel(**inputs):
    import numpy as np
    import concourse.bacc as bacc
    from concourse.bass_utils import run_bass_kernel_spmd as run

    nc = bacc.Bacc("TRN2", target_bir_lowering=False, num_devices=1)
    arrays = {"x_dram": np.ascontiguousarray(inputs["x"]), "ctx_dram": np.ascontiguousarray(inputs["ctx_768"])}
    for name in _W:
        arrays[f"{name}_dram"] = np.stack([np.asarray(inputs[f"L{i}_xattn_{name}"]) for i in range(L)])
    b1 = arrays["ff_b1_dram"].reshape(L, 2, FM, P)
    arrays["ff_b1_dram"] = np.ascontiguousarray(b1.transpose(0, 3, 1, 2))
    aps = {name: nc.dram_tensor(name, a.shape, mybir.dt.from_np(a.dtype), kind="ExternalInput").ap()
           for name, a in arrays.items()}
    out = nc.dram_tensor("out_dram", (B, T, D), F32, kind="ExternalOutput").ap()
    blocks_kernel(nc, aps["x_dram"], aps["ctx_dram"], {name: aps[f"{name}_dram"] for name in _W}, out)
    return run(nc, [arrays], core_ids=[0]).results[0]["out_dram"]
```

```python
from contextlib import ExitStack

import concourse.bass as bass
from concourse import mybir

F32 = mybir.dt.float32
F32R = mybir.dt.float32r
ALU = mybir.AluOpType
ACT = mybir.ActivationFunctionType
AX_X = mybir.AxisListType.X

P = 128
B, T, D = 4, 512, 320
L = 2
J, C = 1601, 192
H, DH = 20, 16
F = 4 * D
EPS = 1e-5
HG = 4
G = H // HG
TT = T // P
KC = 3
DC = [(c * P, min(P, D - c * P)) for c in range(KC)]
CC = C // 2
JP = J + 1
JT = (J + P - 1) // P
JN = [(n, min(512, JP - n)) for n in range(0, JP, 512)]
FM = F // P
RING = 3
DRING = 4
QK_RING = 3


class Attn:

    def __init__(self, keys, key_rows, units, pieces, mt_at, mt_last, stage, slot0, kt0, num0):
        self.keys = keys
        self.kt = len(key_rows)
        self.key_rows = key_rows
        self.units = units
        self.pieces = pieces
        self.turn_at, self.spread_at = ([p[2] for p in pieces].index(kind) for kind in ("turn", "spread"))
        self.mt_at = mt_at
        self.mt_last = mt_last
        self.stage = stage
        self.slots = 4 * self.kt + 2
        self.slot0, self.kt0, self.num0 = slot0, kt0, num0
        self.first = slot0 + 2
        self.turned = self.first - self.slots + 4 * (mt_at + 1)
        self.scored = self.first - self.slots - (2 if mt_at == self.kt - 1 else 0)

    def bank_at(self, g):
        return g * (2 * len(self.pieces)) + (POS[self.stage] + 2 * len(self.units))


HALF = 802
SELF_UNITS = [(h, (q, q + 1), 0, T) for h in range(HG) for q in range(0, TT, 2)]
CROSS_UNITS = [(h, (q,), n, min(HALF, JP - n)) for h in range(HG) for q in range(TT) for n in (0, HALF)]
SELF_PIECES = [(0, 1, "unit"), (0, 3, "unit"), (0, 4, "turn"), (1, 0, "unit"), (1, 1, "spread"), (1, 3, "unit"),
               (1, 4, "unit"), (2, 1, "unit"), (2, 3, "unit"), (3, 1, "unit")]
CROSS_PIECES = [(0, 3, "turn"), (1, 0, "spread"), (1, 3, "unit"), (1, 4, "unit")]
CROSS_PIECES += [(k, place, "unit") for k in range(2, 12) for place in (1, 3, 4)]
SELF = Attn(T, [P] * TT, SELF_UNITS, SELF_PIECES, 3, True, "max1", 0, 0, 0)
CROSS = Attn(JP, [min(P, J - k * P) for k in range(JT)], CROSS_UNITS, CROSS_PIECES, 12, False,
             "max2", G * SELF.slots, G * SELF.kt, G)
assert all(len(a.pieces) == len(a.units) + 2 for a in (SELF, CROSS))
SLOTS = G * (SELF.slots + CROSS.slots)
KTS = G * (SELF.kt + CROSS.kt)
GROUPS = 2 * G
KT_CREDIT = 2 + TT
assert SELF.slots % RING == 0 and CROSS.slots % RING == 0 and SELF.kt0 % 2 == 0 and CROSS.kt0 % 2 == 0

STAGES = [("t1", KC, 1, 0), ("q1", KC, 1, 0), ("k1", KC, 1, 0), ("v1", TT, 1, 3),
          ("max1", G * len(SELF_UNITS) + 2 * (G + 1), 2, 0), ("o1", TT, 1, 0), ("t2", KC, 1, 0), ("q2", KC, 1, 0),
          ("tc", 2 * len(JN), 1, 0), ("k2", KC * len(JN), 1, 0), ("v2", JT, 1, 1),
          ("max2", G * len(CROSS_UNITS) + 2 * (G + 1), 2, 0), ("o2", TT, 1, 0), ("t3", KC, 1, 1), ("ff1", FM, 2, 0),
          ("ff2", TT, 1, 0)]
POS, COUNT, WIDTH, SKIP = {}, {}, {}, {}
BANKS = 0
for _name, _n, _w, _skip in STAGES:
    POS[_name], COUNT[_name], WIDTH[_name], SKIP[_name] = BANKS, _n, _w, _skip
    BANKS += _n * _w + _skip
assert BANKS % DRING == 0 and all(POS[s] % DRING == 0 for s in ("max1", "max2", "ff1"))


def done(stage, i=None):
    return POS[stage] + (COUNT[stage] if i is None else i + 1) * WIDTH[stage]


def begin(stage, i):
    return POS[stage] + (i + 1) * WIDTH[stage]


def step(stage, i):
    return WIDTH[stage] + (SKIP[stage] if i == COUNT[stage] - 1 else 0)


KEY_JOBS = [(c, n, cols) for n, cols in JN for c in range(KC)]
ROW_JOBS = [(c, 0, T) for c in range(KC)]
QK0 = {"q1": 0, "k1": KC, "q2": 2 * KC, "k2": 3 * KC}
QK_TILES = 3 * KC + len(KEY_JOBS)
assert QK_TILES % QK_RING == 0
STACK = {"q": (0, 1, 0), "k": (0, 0, 1)}
STACK_ROW = (0, DH, 3 * DH)
MAX_ROW = 2 * DH
ROWS = 4 * DH
STAGE_DMAS = 3
STORE_DMAS = 3
SMALL = ["q1", "k1", "v1", "q2"]


def blocks_kernel(nc, x, ctx_in, w, out):
    es = ExitStack()
    with es:
        def sb(name, shape, dt=F32):
            return es.enter_context(nc.sbuf_tensor(name, shape, dt))

        def sem(name):
            return es.enter_context(nc.semaphore(name))

        wsq = {n: sb("w_" + n, [P, KC, D]) for n in SMALL}
        wo = {n: sb("w_" + n, [P, G, D]) for n in ("o1", "o2")}
        wctx = {n: sb("w_" + n, [CC, 2, D]) for n in ("k2", "v2")}
        wff1 = sb("wff1", [P, 2, KC, 2, P])
        wff2 = sb("wff2", [P, FM, D])
        brow = sb("brow", [P, 3, D])
        gcol = sb("gcol", [P, 3, 2, KC])
        b1col = sb("b1col", [P, 2, FM])
        X = sb("X", [P, TT, D])
        XN = sb("XN", [P, TT, D])
        HN = sb("HN", [P, TT, D])
        hT = sb("hT", [P, KC, T])
        stats = sb("stats", [P, TT, 6])
        mv = sb("mv", [P, TT, 2])
        rstd = sb("rstd", [P, 2, TT])
        CT = sb("CT", [P, JT, C])
        cT_OA = sb("cT_OA", [P, 2 * JP])
        cT = cT_OA[0:CC, :].rearrange("p (c n) -> p c n", c=2)
        OA = cT_OA[:, 0:(G + 1) * T].rearrange("p (g n) -> p g n", g=G + 1)
        V_uT = sb("V_uT", [P, FM * T])
        V = V_uT[:, 0:JT * D].rearrange("p (k n) -> p k n", k=JT)
        uT = V_uT[:, :].rearrange("p (m n) -> p m n", m=FM)
        KS = sb("KS", [P, 2, 2, JP], F32R)
        QS = sb("QS", [P, 2, HG, T], F32R)
        VS = sb("VS", [P, 2, JT, HG, 32])
        ET = sb("ET", [P, 2, HG, T])
        QK = ET[:, :, :, :].rearrange("p a h n -> p (a h) n")
        OU = sb("OU", [P, T])
        RD = sb("RD", [P, TT, HG])
        mx = sb("mx", [P, TT, HG, 2])
        nm = sb("nm", [P, TT, HG])
        MS = sb("MS", [P, TT, 2, 64 + MAX_ROW + 2], F32R)
        ident = sb("ident", [P, P])
        identr = sb("identr", [P, P], F32R)
        sel = sb("sel", [P, P])
        minus_half = sb("minus_half", [P, TT])

        pd = [es.enter_context(nc.psum_tensor(f"pd{i}", [P, 2, 512], F32)) for i in range(DRING // 2)]
        pr = [es.enter_context(nc.psum_tensor(f"pr{i}", [P, 512], F32)) for i in range(RING)]
        po = es.enter_context(nc.psum_tensor("po", [P, 512], F32))

        def bank(pos):
            return pd[(pos % DRING) // 2][:, pos % 2, :]

        def split_tile(q, part, rows, cols):
            return QK[0:rows, 2 * (q % QK_RING) + part, 0:cols]

        scr = {k: nc.dram_tensor("scr_" + k, (H, ROWS, JP if k == "k2" else T), F32,
                                 kind="Internal").ap() for k in ("q1", "k1", "q2", "k2")}

        zeroed = sem("zeroed")
        consts = sem("consts")
        scratch_set = sem("scratch_set")
        identr_set = sem("identr_set")
        x_copied = sem("x_copied")
        w_in = sem("w_in")
        x_in = sem("x_in")
        ctx_loaded = sem("ctx_loaded")
        wff1_in = [sem(f"wff1_in{i}") for i in range(2)]
        bank_ready = sem("bank_ready")
        bank_free = sem("bank_free")
        slot_ready = sem("slot_ready")
        slot_free = sem("slot_free")
        high_ready = sem("high_ready")
        stored = [sem(f"stored{i}") for i in range(QK_RING)]
        stats_done = sem("stats_done")
        mean_done = sem("mean_done")
        var_done = sem("var_done")
        rstd_done = sem("rstd_done")
        norm_done = sem("norm_done")
        bias_done = sem("bias_done")
        staged = [sem(f"staged{par}") for par in range(2)]
        vals_staged = sem("vals_staged")
        keys_done = sem("keys_done")
        sums_out = sem("sums_out")
        max_steps = sem("max_steps")
        gate_done = sem("gate_done")
        x_stored = sem("x_stored")
        passed = sem("passed")

        block = es.enter_context(nc.Block())

        def alone(eng):
            eng.sem_inc(passed, 1)

        def pairs(eng, group):
            with eng.Fori(0, G // 2) as i:
                group(i * 2, 0)
                group(i * 2 + 1, 1)
            group(G - 1, 0)

        W_LOADS = 4 * KC + 2 * HG + 2 + 3 + 6 * KC + 2

        cleared = [t[:, :, :] for t in (*wsq.values(), *wo.values(), hT)]
        cleared += [wff1[:, :, :, :, :], VS[:, :, :, :, :], QS[:, :, :, :].bitcast(F32), MS[:, :, :, :].bitcast(F32),
                    V_uT[:, :], ident[:, :], sel[:, :]]
        CONSTS = 6

        @block.sync
        def _(sp):
            sp.dma_start(out.rearrange("b (s p) d -> (b s) (p d)", p=32),
                         x.rearrange("b (s p) d -> (b s) (p d)", p=32)).then_inc(x_copied, 16)
            for s in stored:
                sp.sem_inc(s, 16 * STORE_DMAS)
            sp.sem_inc(x_stored, 16)
            sp.wait_ge(x_copied, 16)
            sp.wait_ge(consts, CONSTS)
            ones = CT[0:2, :, :].rearrange("p t (a c) -> p a (t c)", a=1)
            zeros = V_uT[0:DH, :].rearrange("p (a n) -> p a n", a=1)
            for k in scr:
                n = scr[k].shape[2]
                for r, src, rows in ((MAX_ROW, zeros, DH),) if k[0] == "q" else (
                        (MAX_ROW, ones, 2), (MAX_ROW + 2, zeros, DH - 2)):
                    sp.dma_start(scr[k][:, r:r + rows, :].rearrange("h r n -> r h n"),
                                 src[0:rows, :, 0:n].to_broadcast([rows, H, n])).then_inc(scratch_set, 16)
            sp.wait_ge(scratch_set, 16 * 6)

            def load_entry(b):
                full = (JT - 1) * P
                sp.dma_start(XN[:, :, :], out[bass.ds(b, 1)].rearrange("b (t p) d -> p (b t) d", p=P)
                             ).then_inc(x_in, 16)
                sp.dma_start(CT[:, 0:JT - 1, :], ctx_in[bass.ds(b, 1), 0:full, :].rearrange(
                    "b (t p) c -> p (b t) c", p=P)).then_inc(ctx_loaded, 16)
                sp.dma_start(CT[0:J - full, JT - 1, :], ctx_in[bass.ds(b, 1), full:J, :].rearrange(
                    "b p c -> (b p) c")).then_inc(ctx_loaded, 16)

            load_entry(0)
            with sp.Fori(0, L) as l:
                def load(dst, src):
                    sp.dma_start(dst, src).then_inc(w_in, 16)

                def layer(name):
                    a = w[name]
                    return a[bass.ds(l, 1)].rearrange(
                        "l " + " ".join("abc"[:len(a.shape) - 1]) + " -> (l a) " + " ".join("bc"[:len(a.shape) - 2]))

                for i in range(3):
                    for j, k in enumerate("gb"):
                        for c, (r, m) in enumerate(DC):
                            load(gcol[0:m, i, j, c:c + 1], layer(f"n{i + 1}_{k}")[r:r + m].rearrange(
                                "(p a) -> p a", a=1))
                for k in SMALL:
                    for c, (r, m) in enumerate(DC):
                        load(wsq[k][0:m, c, :], layer(k)[r:r + m, :])
                for i, k in enumerate(("o1_b", "o2_b", "ff_b2")):
                    load(brow[:, i, :], w[k][bass.ds(l, 1), :].partition_broadcast(P))
                for k in ("o1", "o2"):
                    src = layer(k + "_w").rearrange("(g h d) n -> h d g n", h=HG, d=DH)
                    for h in range(HG):
                        load(wo[k][32 * h:32 * h + DH, :, :], src[h])
                for k in ("k2", "v2"):
                    load(wctx[k][:, :, :], layer(k).rearrange("(c p) n -> p c n", c=2))
                load(b1col[:, :, :], w["ff_b1"][bass.ds(l, 1)].rearrange("l p a m -> (l p) a m"))
                load(wff2[:, :, :], layer("ff_w2").rearrange("(m p) n -> p m n", p=P))
                with sp.Fori(0, B) as b:
                    it = l * B + b
                    entry = out[bass.ds(b, 1)].rearrange("b (t p) d -> p (b t) d", p=P)
                    def store(kind, jobs):
                        for i, (c, n0, cols) in enumerate(jobs):
                            q, (r, m) = QK0[kind] + i, DC[c]
                            sp.wait_ge(bank_free, it * BANKS + DRING + done(kind, i))
                            for k, part in enumerate(STACK[kind[0]]):
                                sp.dma_start(scr[kind][r // DH:(r + m) // DH, STACK_ROW[k]:STACK_ROW[k] + DH, n0:n0 + cols],
                                             split_tile(q, part, m, cols)).then_inc(stored[q % QK_RING], 16)

                    def wait_stored(tiles):
                        for s in range(QK_RING):
                            n = (tiles - s + QK_RING - 1) // QK_RING
                            sp.wait_ge(stored[s], it * (16 * STORE_DMAS * QK_TILES // QK_RING) + 16 * STORE_DMAS * (1 + n))
                            alone(sp)

                    def attention(a, qs, ks):
                        def group(g, par):
                            if not (isinstance(g, int) and g == 0):
                                sp.wait_ge(slot_ready, it * SLOTS + g * a.slots + (a.scored + 1))
                            keys = ks[bass.ds(g * HG, HG), :, :]
                            sp.dma_start(KS[:, par, :, 0:a.keys].bitcast(F32),
                                         keys.rearrange("(b e) r n -> (e r) b n", e=2)).then_inc(staged[par], 16)
                            for e in range(2):
                                sp.dma_start(QS[64 * e:64 * e + ROWS, par, e::2, :].bitcast(F32),
                                             qs[bass.ds(g * HG + e, HG // 2, 2), :, :].rearrange("h r n -> r h n")
                                             ).then_inc(staged[par], 16)
                        group(0, 0)
                        with sp.Fori(0, G // 2) as i:
                            group(i * 2 + 1, 1)
                            group(i * 2 + 2, 0)

                    def load_ff1(m, a):
                        for v in range(2):
                            for c, (r, rows) in enumerate(DC):
                                sp.dma_start(wff1[0:rows, a, c, v, :],
                                             w["ff_w1"][bass.ds(l, 1), r:r + rows, bass.ds(m * P + v * F, P)
                                                        ].rearrange("l p n -> (l p) n")).then_inc(wff1_in[a], 16)

                    store("q1", ROW_JOBS)
                    store("k1", ROW_JOBS)
                    wait_stored(QK0["q2"])
                    attention(SELF, scr["q1"], scr["k1"])
                    store("q2", ROW_JOBS)
                    store("k2", KEY_JOBS)
                    wait_stored(QK_TILES)
                    sp.wait_ge(bias_done, it * (3 * TT) + TT)
                    alone(sp)
                    sp.wait_ge(bank_free, it * BANKS + DRING + done("tc"))
                    alone(sp)
                    load_entry((b + 1) % B)
                    for a in range(2):
                        load_ff1(a, a)
                    attention(CROSS, scr["q2"], scr["k2"])
                    with sp.Fori(0, FM // 2 - 1) as i:
                        for a in range(2):
                            m = i * 2 + a
                            sp.wait_ge(bank_ready, it * BANKS + m * 2 + (POS["ff1"] + 2))
                            load_ff1(m + 2, a)
                    sp.wait_ge(bank_free, it * BANKS + DRING + BANKS)
                    sp.dma_start(entry, X[:, :, :]).then_inc(x_stored, 16)
                    sp.wait_ge(x_stored, it * 16 + 32)
                    alone(sp)
            sp.wait_ge(x_in, 16 * (L * B + 1))
            sp.wait_ge(ctx_loaded, 32 * (L * B + 1))

        @block.gpsimd
        def _(pool):
            gp = nc.gpsimd
            for t in cleared:
                gp.memset(t, 0.0).then_inc(zeroed, 1)
            pool.sem_inc(vals_staged, 1)
            gp.memset(minus_half[:, :], -0.5).then_inc(consts, 1)
            gp.memset(OU[:, :], 1.0).then_inc(consts, 1)
            gp.memset(CT[:, :, :], 1.0).then_inc(consts, 1)
            pool.wait_ge(zeroed, len(cleared))
            gp.affine_select(out=ident[:, :], in_=ident[:, :], compare_op=ALU.not_equal, fill=1.0,
                             base=0, pattern=[[-1, P]], channel_multiplier=1).then_inc(consts, 1)
            of_head = sel[:, :].rearrange("p (a m) -> p a m", a=HG)
            gp.affine_select(out=of_head, in_=of_head, compare_op=ALU.not_equal, fill=1.0,
                             base=-DH, pattern=[[-32, HG], [0, 32]], channel_multiplier=1).then_inc(consts, 1)
            gp.memset(VS[:, :, :, :, DH:DH + 1], 1.0).then_inc(consts, 1)
            with pool.Fori(0, L) as l:
                pool.wait_ge(w_in, l * (16 * W_LOADS) + 16 * W_LOADS)
                alone(pool)
                with pool.Fori(0, B) as b:
                    it = l * B + b

                    def norm_scale(i):
                        pool.wait_ge(mean_done, it * (3 * TT) + TT * (i + 1))
                        alone(pool)
                        gp.tensor_scalar(rstd[:, 0, :], mv[:, :, 1], EPS, None, ALU.add).then_inc(var_done, 1)
                        pool.wait_ge(var_done, it * 3 + i + 1)
                        gp.tensor_tensor(rstd[:, 1, :], rstd[:, 0, :], minus_half[:, :], ALU.pow
                                         ).then_inc(rstd_done, 1)
                        pool.wait_ge(norm_done, it * (3 * TT) + TT * (i + 1))
                        if i == 0:
                            pool.wait_ge(x_stored, it * 16 + 16)
                        for t in range(TT):
                            gp.tensor_tensor(X[:, t, :], (X if i else XN)[:, t, :], brow[:, i, :], ALU.add
                                             ).then_inc(bias_done, 1)

                    def attention(a, stage):
                        def stage_values(g, par):
                            pool.wait_ge(keys_done, it * KTS + g * a.kt + (KT_CREDIT + a.kt0 - a.kt))
                            alone(pool)
                            for k in range(0, a.kt, 4):
                                n = min(4, a.kt - k)
                                ins = gp.tensor_copy(VS[:, par, k:k + n, :, 0:DH],
                                                     V[:, k:k + n, bass.ds(g * (HG * DH), HG * DH)].rearrange(
                                                         "p k (h d) -> p k h d", h=HG))
                            ins.then_inc(vals_staged, 1)

                        pool.wait_ge(bank_free, it * BANKS + DRING + done(stage))
                        alone(pool)
                        pairs(pool, stage_values)

                    norm_scale(0)
                    attention(SELF, "v1")
                    norm_scale(1)
                    attention(CROSS, "v2")
                    norm_scale(2)

        @block.scalar
        def _(act):
            act.sem_inc(slot_free, RING)
            act.sem_inc(sums_out, 1)
            with act.Fori(0, L) as l:
                act.wait_ge(w_in, l * (16 * W_LOADS) + 16 * W_LOADS)
                with act.Fori(0, B) as b:
                    it = l * B + b

                    def high(kind, jobs, scale):
                        for i, (c, n0, cols) in enumerate(jobs):
                            q, m = QK0[kind] + i, DC[c][1]
                            act.wait_ge(bank_ready, it * BANKS + done(kind, i))
                            act.wait_ge(stored[q % QK_RING], it * (16 * STORE_DMAS * QK_TILES // QK_RING) + 16 * STORE_DMAS * (1 + q // QK_RING))
                            nc.scalar.activation(split_tile(q, 0, m, cols).bitcast(F32R),
                                                 bank(POS[kind] + i)[0:m, 0:cols], ACT.Copy, scale=scale
                                                 ).then_inc(high_ready, 1)

                    def attention(a):
                        def turn(par, r, slot):
                            for pair in range(2):
                                act.wait_ge(slot_ready, it * SLOTS + slot + (pair + 2))
                                for e in range(2):
                                    row = 64 * e + MAX_ROW
                                    ins = nc.scalar.copy(QS[row:row + 2, par, 2 * pair + e, :],
                                                         pr[(r + pair) % RING][row:row + 2, :])
                                ins.then_inc(slot_free, 1)

                        def group(g, par, last=False):
                            r, slot = 2, g * a.slots + a.first
                            for k, m in enumerate(a.key_rows):
                                act.wait_ge(keys_done, it * KTS + g * a.kt + (a.kt0 + k + KT_CREDIT - 1))
                                for h in range(HG):
                                    act.wait_ge(slot_ready, it * SLOTS + slot + 2)
                                    nc.scalar.activation(ET[0:m, (par * a.kt + k) % 2, h, :], pr[r % RING][0:m, :],
                                                         ACT.Exp).then_inc(slot_free, 1)
                                    r, slot = r + 1, slot + 1
                                if k == a.mt_at and not last and not a.mt_last:
                                    turn(1 - par, r, slot)
                                    r, slot = r + 2, slot + 2
                            act.wait_ge(keys_done, it * KTS + g * a.kt + (a.kt0 + a.kt + KT_CREDIT))
                            divided = 4 if last else 2 * (a.spread_at + 1)
                            act.wait_ge(bank_free, it * BANKS + a.bank_at(g) + (divided + DRING))
                            nc.scalar.copy(OU[:, :], po[:, :]).then_inc(sums_out, 1)
                            if a.mt_last and not last:
                                turn(1 - par, r, slot)

                        turn(0, 0, a.slot0)
                        with act.Fori(0, G // 2) as i:
                            group(i * 2, 0)
                            group(i * 2 + 1, 1)
                        group(G - 1, 0, last=True)

                    high("q1", ROW_JOBS, DH ** -0.5)
                    high("k1", ROW_JOBS, 1.0)
                    attention(SELF)
                    high("q2", ROW_JOBS, DH ** -0.5)
                    high("k2", KEY_JOBS, 1.0)
                    attention(CROSS)
                    with act.Fori(0, FM // 2) as i:
                        for j in range(2):
                            m = i * 2 + j
                            act.wait_ge(bank_ready, it * BANKS + m * 2 + (POS["ff1"] + 1))
                            act.wait_ge(bank_free, it * BANKS + m * 2 + (POS["ff1"] + DRING - 2))
                            nc.scalar.activation(ET[:, 0, j, :], bank(2 * j), ACT.Gelu,
                                                 bias=b1col[:, 1, bass.ds(m, 1)]).then_inc(gate_done, 1)

        @block.vector
        def _(dve):
            v = nc.vector
            dve.sem_inc(bank_free, DRING)
            dve.wait_ge(consts, CONSTS)
            v.tensor_copy(identr[:, :], ident[:, :]).then_inc(identr_set, 1)
            with dve.Fori(0, L) as l:
                dve.wait_ge(w_in, l * (16 * W_LOADS) + 16 * W_LOADS)
                alone(dve)
                with dve.Fori(0, B) as b:
                    it = l * B + b

                    def normalise(i):
                        src = X if i else XN
                        for t in range(TT):
                            v.bn_stats(stats[:, t, :], src[:, t, :]).then_inc(stats_done, 1)
                        for t in range(TT):
                            dve.wait_ge(stats_done, it * (3 * TT) + TT * i + t + 1)
                            alone(dve)
                            v.bn_aggr(mv[:, t, :], stats[:, t, :]).then_inc(mean_done, 1)
                        dve.wait_ge(rstd_done, it * 3 + i + 1)
                        for t in range(TT):
                            v.tensor_scalar(HN[:, t, :], src[:, t, :], mv[:, t, 0:1], rstd[:, 1, t:t + 1],
                                            ALU.subtract, ALU.mult).then_inc(norm_done, 1)
                        stage = f"t{i + 1}"
                        for c, (r, m) in enumerate(DC):
                            dve.wait_ge(bank_ready, it * BANKS + done(stage, c))
                            v.tensor_scalar(hT[0:m, c, :], bank(POS[stage] + c)[0:m, :], gcol[0:m, i, 0, c:c + 1],
                                            gcol[0:m, i, 1, c:c + 1], ALU.mult, ALU.add
                                            ).then_inc(bank_free, step(stage, c))

                    def low(kind, jobs, scale):
                        for i, (c, n0, cols) in enumerate(jobs):
                            q, m = QK0[kind] + i, DC[c][1]
                            dve.wait_ge(high_ready, it * QK_TILES + q + 1)
                            v.scalar_tensor_tensor(split_tile(q, 1, m, cols), bank(POS[kind] + i)[0:m, 0:cols],
                                                   scale, split_tile(q, 0, m, cols), ALU.mult, ALU.subtract
                                                   ).then_inc(bank_free, step(kind, i))

                    def take_values(stage, rows, groups):
                        dve.wait_ge(vals_staged, it * GROUPS + groups + 1)
                        for k, m in enumerate(rows):
                            dve.wait_ge(bank_ready, it * BANKS + done(stage, k))
                            v.tensor_copy(V[0:m, k, :], bank(POS[stage] + k)[0:m, 0:D]
                                          ).then_inc(bank_free, step(stage, k))

                    def attention(a):
                        def reduce(u, at, i):
                            h, qts, n0, cols = a.units[u]
                            dve.wait_ge(bank_ready, it * BANKS + at + (2 * i + 2))
                            both = pd[i % 2]
                            if a is SELF:
                                v.reduce_max(mx[:, qts[0]:qts[0] + 2, h, 0], both[:, :, 0:cols], AX_X
                                             ).then_inc(bank_free, 2)
                            else:
                                v.reduce_max(mx[:, qts[0], h, n0 // HALF:n0 // HALF + 1],
                                             both[:, :, :].rearrange("p a n -> p (a n)")[:, 0:cols], AX_X
                                             ).then_inc(bank_free, 2)

                        def minus_maxima(g, end):
                            dve.wait_ge(bank_free, it * BANKS + end + DRING)
                            by_pair = nm[:, :, :].rearrange("p t (b e) -> p t b e", e=2)
                            v.tensor_reduce(nm[:, :, :], mx[:, :, :, 0:1 if a is SELF else 2], AX_X, ALU.max,
                                            negate=True).then_inc(max_steps, 1)
                            dve.wait_ge(max_steps, it * (3 * GROUPS) + g * 3 + (3 * a.num0 + 1))
                            v.tensor_copy(MS[:, :, :, MAX_ROW::64], by_pair).then_inc(max_steps, 1)
                            dve.wait_ge(max_steps, it * (3 * GROUPS) + g * 3 + (3 * a.num0 + 2))
                            v.tensor_tensor(MS[:, :, :, MAX_ROW + 1::64], by_pair,
                                            MS[:, :, :, MAX_ROW::64].bitcast(F32), ALU.subtract
                                            ).then_inc(max_steps, 1)

                        def invert(at, i):
                            dve.wait_ge(bank_ready, it * BANKS + at + (2 * i + 2))
                            v.reciprocal(RD[:, :, :].rearrange("p t h -> p (t h)"), pd[i % 2][:, 0, 0:TT * HG]
                                         ).then_inc(bank_free, 2)

                        def divide(g, at, i):
                            dve.wait_ge(bank_ready, it * BANKS + at + (2 * i + 2))
                            dst = OA[:, G, :] if g is G else OA[:, bass.ds(g, 1), :].rearrange("p g n -> p (g n)")
                            v.tensor_tensor(dst, pd[i % 2][:, 0, :], OU[:, :], ALU.mult).then_inc(bank_free, 2)

                        for u in range(len(a.units)):
                            reduce(u, POS[a.stage], u)
                        minus_maxima(0, done(a.stage, len(a.units) - 1))
                        with dve.Fori(0, G - 1) as g:
                            at, u = a.bank_at(g), 0
                            for i, (_, _, kind) in enumerate(a.pieces):
                                if kind == "turn":
                                    invert(at, i)
                                elif kind == "spread":
                                    divide(g, at, i)
                                else:
                                    reduce(u, at, i)
                                    u += 1
                            minus_maxima(g + 1, at + 2 * len(a.pieces))
                        for g in (G - 1, G):
                            at = a.bank_at(G - 1) + 4 * (g - (G - 1))
                            invert(at, 0)
                            divide(g, at, 1)

                    def add_to_x(stage, biases):
                        for t in range(TT):
                            dve.wait_ge(bias_done, it * (3 * TT) + TT * biases + t + 1)
                            dve.wait_ge(bank_ready, it * BANKS + done(stage, t))
                            v.tensor_tensor(X[:, t, :], bank(POS[stage] + t)[:, 0:D], X[:, t, :], ALU.add
                                            ).then_inc(bank_free, step(stage, t))
                        dve.wait_ge(bank_free, it * BANKS + DRING + done(stage))
                        alone(dve)

                    dve.wait_ge(x_in, it * 16 + 16)
                    normalise(0)
                    low("q1", ROW_JOBS, DH ** -0.5)
                    low("k1", ROW_JOBS, 1.0)
                    take_values("v1", SELF.key_rows, 0)
                    attention(SELF)
                    add_to_x("o1", 0)
                    normalise(1)
                    low("q2", ROW_JOBS, DH ** -0.5)
                    for c in range(2):
                        for i, (n0, cols) in enumerate(JN):
                            j = c * len(JN) + i
                            dve.wait_ge(bank_ready, it * BANKS + done("tc", j))
                            if n0 + cols > J:
                                v.tensor_copy(cT[:, c, J:JP], bank(POS["tc"] + j)[0:CC, J - 1 - n0:J - n0])
                                cols = J - n0
                            v.tensor_copy(cT[:, c, n0:n0 + cols], bank(POS["tc"] + j)[0:CC, 0:cols]
                                          ).then_inc(bank_free, step("tc", j))
                    low("k2", KEY_JOBS, 1.0)
                    take_values("v2", CROSS.key_rows, G)
                    attention(CROSS)
                    add_to_x("o2", 1)
                    normalise(2)
                    with dve.Fori(0, FM // 2) as i:
                        for j in range(2):
                            m = i * 2 + j
                            dve.wait_ge(bank_ready, it * BANKS + m * 2 + (POS["ff1"] + 2))
                            dve.wait_ge(gate_done, it * FM + m + 1)
                            v.scalar_tensor_tensor(uT[:, bass.ds(m, 1), :].rearrange("p m n -> p (m n)"),
                                                   bank(2 * j + 1), b1col[:, 0, bass.ds(m, 1)], ET[:, 0, j, :],
                                                   ALU.add, ALU.mult).then_inc(bank_free, 2)
                    add_to_x("ff2", 2)

        @block.tensor
        def _(pe):
            mm = nc.tensor.matmul
            pe.sem_inc(keys_done, KT_CREDIT)
            pe.sem_inc(slot_ready, 1)
            pe.wait_ge(zeroed, len(cleared))
            pe.wait_ge(consts, CONSTS)
            pe.wait_ge(identr_set, 1)
            with pe.Fori(0, L) as l:
                pe.wait_ge(w_in, l * (16 * W_LOADS) + 16 * W_LOADS)
                alone(pe)
                with pe.Fori(0, B) as b:
                    it = l * B + b

                    def turn_norm(i):
                        stage = f"t{i + 1}"
                        for c, (r, m) in enumerate(DC):
                            pe.wait_ge(bank_free, it * BANKS + begin(stage, c))
                            alone(pe)
                            for t in range(TT):
                                if c == 0:
                                    pe.wait_ge(norm_done, it * (3 * TT) + TT * i + t + 1)
                                ins = nc.tensor.transpose(bank(POS[stage] + c)[0:m, t * P:(t + 1) * P],
                                                          HN[:, t, r:r + m], ident[:, :])
                            ins.then_inc(bank_ready, step(stage, c))

                    def project(kind):
                        for c, (r, m) in enumerate(DC):
                            pe.wait_ge(bank_free, it * BANKS + begin(kind, c))
                            for k in range(KC):
                                ins = mm(bank(POS[kind] + c)[0:m, :], wsq[kind][:, k, r:r + m], hT[:, k, :],
                                         start=k == 0, stop=k == KC - 1)
                            ins.then_inc(bank_ready, step(kind, c))

                    def attention(a):
                        def unit(par, u, at, i):
                            h, qts, n0, cols = a.units[u]
                            pe.wait_ge(bank_free, it * BANKS + at + (2 * i + 2))
                            if a is SELF:
                                parts = [(q, j, 0, cols) for j, q in enumerate(qts)]
                            else:
                                parts = [(qts[0], 0, n0, 512), (qts[0], 1, n0 + 512, cols - 512)]
                            for q, j, n, width in parts:
                                ins = mm(pd[i % 2][:, j, 0:width], QS[:, par, h, q * P:(q + 1) * P],
                                         KS[:, par, h // 2, n:n + width], start=True, stop=True)
                            ins.then_inc(bank_ready, 2)

                        def wait_staged(i, par):
                            groups = (G + 1 - par) // 2
                            pe.wait_ge(staged[par], it * (16 * STAGE_DMAS * 2 * groups) + i * (16 * STAGE_DMAS)
                                       + 16 * STAGE_DMAS * (1 + (groups if a is CROSS else 0)))
                            alone(pe)

                        def turn_max(g, r, slot):
                            pe.wait_ge(max_steps, it * (3 * GROUPS) + g * 3 + 3 * (a.num0 + 1))
                            for pair in range(2):
                                pe.wait_ge(slot_free, it * SLOTS + slot + (pair + 1))
                                for q in range(TT):
                                    ins = mm(pr[(r + pair) % RING][0:64 + MAX_ROW + 2, q * P:(q + 1) * P],
                                             MS[:, q, pair, :], identr[:, :], start=True, stop=True)
                                ins.then_inc(slot_ready, 1)

                        def weigh(g, par, k, last):
                            m = a.key_rows[k]
                            for h in range(HG):
                                n = 4 * (k + 1) + (2 if k > a.mt_at and not last else 0)
                                if h == 0:
                                    pe.wait_ge(slot_free, it * SLOTS + g * a.slots + (a.first + n + RING))
                                ins = mm(po[32 * h:32 * h + 32, :], VS[0:m, par, k, h, :],
                                         ET[0:m, (par * a.kt + k) % 2, h, :], start=k == 0, stop=k == a.kt - 1)
                            ins.then_inc(keys_done, 1)

                        def turn_divisors(g, at, i):
                            pe.wait_ge(sums_out, it * GROUPS + g + (a.num0 + 1))
                            pe.wait_ge(bank_free, it * BANKS + at + (2 * i + 2))
                            for q in range(TT):
                                ins = mm(pd[i % 2][:, 0, q * HG:(q + 1) * HG], OU[:, q * P:(q + 1) * P], sel[:, ::32],
                                         start=True, stop=True)
                            ins.then_inc(bank_ready, 2)

                        def spread_reciprocals(at, turn_at, i):
                            pe.wait_ge(bank_free, it * BANKS + at + max(2 * turn_at + 2 + DRING, 2 * i + 2))
                            for q in range(TT):
                                for h in range(HG):
                                    ins = mm(pd[i % 2][32 * h:32 * h + 32, 0, q * P:(q + 1) * P],
                                             RD[:, q, h:h + 1].to_broadcast([P, 32]), ident[:, :],
                                             start=True, stop=True)
                            ins.then_inc(bank_ready, 2)

                        def group(i2, par, last=False):
                            g = i2 * 2 + par
                            r, slot = 2, g * a.slots + a.first
                            at = a.bank_at(g)
                            nxt = g + 1

                            def pieces(k, place):
                                for i, (at_k, at_place, kind) in enumerate(a.pieces):
                                    if (at_k, at_place) != (k, place):
                                        continue
                                    if kind == "turn":
                                        turn_divisors(g, at, 0 if last else i)
                                    elif kind == "spread":
                                        spread_reciprocals(at, 0 if last else a.turn_at, 1 if last else i)
                                    elif not last:
                                        u = [p[2] for p in a.pieces[:i]].count("unit")
                                        if u == 0:
                                            wait_staged(i2 + par, 1 - par)
                                        unit(1 - par, u, at, i)

                            for k, m in enumerate(a.key_rows):
                                for h in range(HG):
                                    if k == 0 and h % 2 == 0:
                                        pe.wait_ge(slot_free, it * SLOTS + g * a.slots + (a.turned + h // 2 + 1 + RING))
                                        alone(pe)
                                    pe.wait_ge(slot_free, it * SLOTS + slot + 1)
                                    mm(pr[r % RING][0:m, :], KS[:, par, h // 2, k * P:k * P + m], QS[:, par, h, :],
                                       start=True, stop=True).then_inc(slot_ready, 1)
                                    r, slot = r + 1, slot + 1
                                    pieces(k, h)
                                if k == 1:
                                    pe.wait_ge(vals_staged, it * GROUPS + g + (a.num0 + 2))
                                if k:
                                    weigh(g, par, k - 1, last)
                                pieces(k, 4)
                                if k == a.mt_at and not last and not a.mt_last:
                                    turn_max(nxt, r, slot)
                                    r, slot = r + 2, slot + 2
                            weigh(g, par, a.kt - 1, last)
                            if a.mt_last and not last:
                                turn_max(nxt, r, slot)
                            if last:
                                turn_divisors(G, at + 4, 0)
                                spread_reciprocals(at + 4, 0, 1)

                        wait_staged(0, 0)
                        for u in range(len(a.units)):
                            unit(0, u, POS[a.stage], u)
                        turn_max(0, 0, a.slot0)
                        pe.wait_ge(slot_free, it * SLOTS + (a.first + RING))
                        alone(pe)
                        with pe.Fori(0, G // 2) as i:
                            group(i, 0)
                            group(i, 1)
                        group(G // 2, 0, last=True)

                    def project_out(kind):
                        pe.wait_ge(bank_free, it * BANKS + (DRING + POS[kind]))
                        for t in range(TT):
                            pe.wait_ge(bank_free, it * BANKS + begin(kind, t))
                            for g in range(G):
                                ins = mm(bank(POS[kind] + t)[:, 0:D], OA[:, g + 1, t * P:(t + 1) * P], wo[kind][:, g, :],
                                         start=g == 0, stop=g == G - 1)
                            ins.then_inc(bank_ready, step(kind, t))

                    turn_norm(0)
                    pe.wait_ge(bank_free, it * BANKS + (DRING + done("t1")))
                    project("q1")
                    project("k1")
                    for t in range(TT):
                        pe.wait_ge(bank_free, it * BANKS + begin("v1", t))
                        for k in range(KC):
                            ins = mm(bank(POS["v1"] + t)[:, 0:D], hT[:, k, t * P:(t + 1) * P], wsq["v1"][:, k, :],
                                     start=k == 0, stop=k == KC - 1)
                        ins.then_inc(bank_ready, step("v1", t))
                    attention(SELF)
                    project_out("o1")
                    turn_norm(1)
                    pe.wait_ge(bank_free, it * BANKS + (DRING + done("t2")))
                    project("q2")
                    pe.wait_ge(ctx_loaded, it * 32 + 32)
                    for c in range(2):
                        for i, (n0, cols) in enumerate(JN):
                            j = c * len(JN) + i
                            pe.wait_ge(bank_free, it * BANKS + begin("tc", j))
                            for k in range(n0 // P, min(JT, n0 // P + 4)):
                                m = CROSS.key_rows[k]
                                ins = nc.tensor.transpose(bank(POS["tc"] + j)[0:CC, k * P - n0:k * P - n0 + m],
                                                          CT[0:m, k, c * CC:(c + 1) * CC], ident[0:m, 0:m])
                            ins.then_inc(bank_ready, step("tc", j))
                    pe.wait_ge(bank_free, it * BANKS + (DRING + done("tc")))
                    for j, (c, n0, cols) in enumerate(KEY_JOBS):
                        r, m = DC[c]
                        pe.wait_ge(bank_free, it * BANKS + begin("k2", j))
                        for k in range(2):
                            ins = mm(bank(POS["k2"] + j)[0:m, 0:cols], wctx["k2"][:, k, r:r + m],
                                     cT[:, k, n0:n0 + cols], start=k == 0, stop=k == 1)
                        ins.then_inc(bank_ready, step("k2", j))
                    for j, m in enumerate(CROSS.key_rows):
                        pe.wait_ge(bank_free, it * BANKS + begin("v2", j))
                        for k in range(2):
                            ins = mm(bank(POS["v2"] + j)[0:m, 0:D], cT[:, k, j * P:j * P + m], wctx["v2"][:, k, :],
                                     start=k == 0, stop=k == 1)
                        ins.then_inc(bank_ready, step("v2", j))
                    attention(CROSS)
                    project_out("o2")
                    turn_norm(2)
                    pe.wait_ge(bank_free, it * BANKS + (DRING + done("t3")))
                    alone(pe)
                    with pe.Fori(0, FM // 2) as i:
                        for j in range(2):
                            m = i * 2 + j
                            pe.wait_ge(wff1_in[j], it * (16 * 2 * KC * (FM // 2)) + i * (16 * 2 * KC) + 16 * 2 * KC)
                            pe.wait_ge(bank_free, it * BANKS + m * 2 + (POS["ff1"] + 2))
                            for side in (1, 0):
                                for k in range(KC):
                                    ins = mm(bank(2 * j + 1 - side), wff1[:, j, k, side, :], hT[:, k, :],
                                             start=k == 0, stop=k == KC - 1)
                                ins.then_inc(bank_ready, 1)
                    pe.wait_ge(bank_free, it * BANKS + (DRING + done("ff1")))
                    for t in range(TT):
                        pe.wait_ge(bank_free, it * BANKS + begin("ff2", t))
                        for m in range(FM):
                            ins = mm(bank(POS["ff2"] + t)[:, 0:D], uT[:, m, t * P:(t + 1) * P], wff2[:, m, :],
                                     start=m == 0, stop=m == FM - 1)
                        ins.then_inc(bank_ready, step("ff2", t))


_W = ["n1_g", "n1_b", "q1", "k1", "v1", "o1_w", "o1_b", "n2_g", "n2_b", "q2", "k2", "v2", "o2_w", "o2_b",
      "n3_g", "n3_b", "ff_w1", "ff_b1", "ff_w2", "ff_b2"]


def kernel(**inputs):
    import numpy as np
    import concourse.bacc as bacc
    from concourse.bass_utils import run_bass_kernel_spmd as run

    nc = bacc.Bacc("TRN2", target_bir_lowering=False, num_devices=1)
    arrays = {"x_dram": np.ascontiguousarray(inputs["x"]), "ctx_dram": np.ascontiguousarray(inputs["ctx_768"])}
    for name in _W:
        arrays[f"{name}_dram"] = np.stack([np.asarray(inputs[f"L{i}_xattn_{name}"]) for i in range(L)])
    b1 = arrays["ff_b1_dram"].reshape(L, 2, FM, P)
    arrays["ff_b1_dram"] = np.ascontiguousarray(b1.transpose(0, 3, 1, 2))
    aps = {name: nc.dram_tensor(name, a.shape, mybir.dt.from_np(a.dtype), kind="ExternalInput").ap()
           for name, a in arrays.items()}
    out = nc.dram_tensor("out_dram", (B, T, D), F32, kind="ExternalOutput").ap()
    blocks_kernel(nc, aps["x_dram"], aps["ctx_dram"], {name: aps[f"{name}_dram"] for name in _W}, out)
    return run(nc, [arrays], core_ids=[0]).results[0]["out_dram"]
```

```python
from contextlib import ExitStack

import concourse.bass as bass
from concourse import mybir

F32 = mybir.dt.float32
F32R = mybir.dt.float32r
ALU = mybir.AluOpType
ACT = mybir.ActivationFunctionType
AX_X = mybir.AxisListType.X

P = 128
B, T, D = 4, 512, 320
L = 2
J, C = 1601, 192
H, DH = 20, 16
F = 4 * D
EPS = 1e-5
HG = 4
G = H // HG
TT = T // P
KC = 3
DC = [(c * P, min(P, D - c * P)) for c in range(KC)]
CC = C // 2
JP = J + 1
JT = (J + P - 1) // P
JN = [(n, min(512, JP - n)) for n in range(0, JP, 512)]
FM = F // P
RING = 3
DRING = 4
QK_RING = 3


class Attn:

    def __init__(self, keys, key_rows, units, pieces, mt_at, mt_last, stage, slot0, kt0, num0):
        self.keys = keys
        self.kt = len(key_rows)
        self.key_rows = key_rows
        self.units = units
        self.pieces = pieces
        self.turn_at, self.spread_at = ([p[2] for p in pieces].index(kind) for kind in ("turn", "spread"))
        self.mt_at = mt_at
        self.mt_last = mt_last
        self.stage = stage
        self.slots = 4 * self.kt + 2
        self.slot0, self.kt0, self.num0 = slot0, kt0, num0
        self.first = slot0 + 2
        self.turned = self.first - self.slots + 4 * (mt_at + 1)
        self.scored = self.first - self.slots - (2 if mt_at == self.kt - 1 else 0)

    def bank_at(self, g):
        return g * (2 * len(self.pieces)) + (POS[self.stage] + 2 * len(self.units))


HALF = 802
SELF_UNITS = [(h, (q, q + 1), 0, T) for h in range(HG) for q in range(0, TT, 2)]
CROSS_UNITS = [(h, (q,), n, min(HALF, JP - n)) for h in range(HG) for q in range(TT) for n in (0, HALF)]
SELF_PIECES = [(0, 1, "unit"), (0, 3, "unit"), (0, 4, "unit"), (1, 2, "turn"), (1, 4, "unit"), (2, 1, "spread"),
               (2, 3, "unit"), (2, 4, "unit"), (3, 1, "unit"), (3, 3, "unit")]
CROSS_PIECES = [(0, 3, "turn"), (1, 0, "spread"), (1, 3, "unit"), (1, 4, "unit")]
CROSS_PIECES += [(k, place, "unit") for k in range(2, 12) for place in (1, 3, 4)]
SELF = Attn(T, [P] * TT, SELF_UNITS, SELF_PIECES, 3, True, "max1", 0, 0, 0)
CROSS = Attn(JP, [min(P, J - k * P) for k in range(JT)], CROSS_UNITS, CROSS_PIECES, 12, False,
             "max2", G * SELF.slots, G * SELF.kt, G)
assert all(len(a.pieces) == len(a.units) + 2 for a in (SELF, CROSS))
SLOTS = G * (SELF.slots + CROSS.slots)
KTS = G * (SELF.kt + CROSS.kt)
GROUPS = 2 * G
KT_CREDIT = 2 + TT
assert SELF.slots % RING == 0 and CROSS.slots % RING == 0 and SELF.kt0 % 2 == 0 and CROSS.kt0 % 2 == 0

STAGES = [("t1", KC, 1, 0), ("q1", KC, 1, 0), ("k1", KC, 1, 0), ("v1", TT, 1, 3),
          ("max1", G * len(SELF_UNITS) + 2 * (G + 1), 2, 0), ("o1", TT, 1, 0), ("tc", 2 * len(JN), 1, 0),
          ("k2", KC * len(JN), 1, 0), ("t2", KC, 1, 0), ("q2", KC, 1, 0), ("v2", JT, 1, 1),
          ("max2", G * len(CROSS_UNITS) + 2 * (G + 1), 2, 0), ("o2", TT, 1, 0), ("t3", KC, 1, 1), ("ff1", FM, 2, 0),
          ("ff2", TT, 1, 0)]
POS, COUNT, WIDTH, SKIP = {}, {}, {}, {}
BANKS = 0
for _name, _n, _w, _skip in STAGES:
    POS[_name], COUNT[_name], WIDTH[_name], SKIP[_name] = BANKS, _n, _w, _skip
    BANKS += _n * _w + _skip
assert BANKS % DRING == 0 and all(POS[s] % DRING == 0 for s in ("max1", "max2", "ff1"))


def done(stage, i=None):
    return POS[stage] + (COUNT[stage] if i is None else i + 1) * WIDTH[stage]


def begin(stage, i):
    return POS[stage] + (i + 1) * WIDTH[stage]


def step(stage, i):
    return WIDTH[stage] + (SKIP[stage] if i == COUNT[stage] - 1 else 0)


KEY_JOBS = [(c, n, cols) for n, cols in JN for c in range(KC)]
ROW_JOBS = [(c, 0, T) for c in range(KC)]
QK0 = {"q1": 0, "k1": KC, "k2": 2 * KC, "q2": 2 * KC + len(KEY_JOBS)}
QK_TILES = 3 * KC + len(KEY_JOBS)
assert QK_TILES % QK_RING == 0
STACK = {"q": (0, 1, 0), "k": (0, 0, 1)}
STACK_ROW = (0, DH, 3 * DH)
MAX_ROW = 2 * DH
ROWS = 4 * DH
STAGE_DMAS = 3
STORE_DMAS = 3
SMALL = ["q1", "k1", "v1", "q2"]


def blocks_kernel(nc, x, ctx_in, w, out):
    es = ExitStack()
    with es:
        def sb(name, shape, dt=F32):
            return es.enter_context(nc.sbuf_tensor(name, shape, dt))

        def sem(name):
            return es.enter_context(nc.semaphore(name))

        w3 = sb("w3", [P, 3, KC, D])
        w_q2 = sb("w_q2", [P, KC, D])
        wsq = {"q1": w3[:, 0], "k1": w3[:, 1], "v1": w3[:, 2], "q2": w_q2}
        wo12 = sb("wo12", [P, 2, G, D])
        wo = {"o1": wo12[:, 0], "o2": wo12[:, 1]}
        w_kv2 = sb("w_kv2", [CC, 2, 2, D])
        wctx = {"k2": w_kv2[:, 0], "v2": w_kv2[:, 1]}
        wff1 = sb("wff1", [P, 2, KC, 2, P])
        wff2 = sb("wff2", [P, FM, D])
        brow = sb("brow", [P, 3, D])
        gcol = sb("gcol", [P, 3, 2, KC])
        b1col = sb("b1col", [P, 2, FM])
        X = sb("X", [P, TT, D])
        XN = sb("XN", [P, TT, D])
        HN = sb("HN", [P, TT, D])
        hT = sb("hT", [P, KC, T])
        stats = sb("stats", [P, TT, 6])
        mv = sb("mv", [P, TT, 2])
        rstd = sb("rstd", [P, 2, TT])
        CT = sb("CT", [P, JT, C])
        cT_OA = sb("cT_OA", [P, 2 * JP])
        cT = cT_OA[0:CC, :].rearrange("p (c n) -> p c n", c=2)
        OA = cT_OA[:, 0:(G + 1) * T].rearrange("p (g n) -> p g n", g=G + 1)
        V_uT = sb("V_uT", [P, FM * T])
        V = V_uT[:, 0:JT * D].rearrange("p (k n) -> p k n", k=JT)
        uT = V_uT[:, :].rearrange("p (m n) -> p m n", m=FM)
        KS = sb("KS", [P, 2, 2, JP], F32R)
        KS_flat = KS[:, :, :, :].rearrange("p a b n -> p (a b n)")
        HS = KS_flat[:, 0:2 * KC * T].rearrange("p (s c n) -> p s c n", s=2, c=KC)
        WS = KS_flat[:, 2 * KC * T:2 * KC * T + 8 * KC * P].rearrange("p (a s c v n) -> p a s c v n", a=2, s=2, c=KC, v=2)
        QS = sb("QS", [P, 2, HG, T], F32R)
        VS = sb("VS", [P, 2, JT, HG, 32])
        ET = sb("ET", [P, 2, HG, T])
        QK = ET[:, :, :, :].rearrange("p a h n -> p (a h) n")
        OU = sb("OU", [P, T])
        RD = sb("RD", [P, TT, HG])
        mx = sb("mx", [P, TT, HG, 2])
        nm = sb("nm", [P, TT, HG])
        MS = sb("MS", [P, TT, 2, 64 + MAX_ROW + 2], F32R)
        ident = sb("ident", [P, P])
        identr = sb("identr", [P, P], F32R)
        sel = sb("sel", [P, P])
        minus_half = sb("minus_half", [P, TT])

        pd = [es.enter_context(nc.psum_tensor(f"pd{i}", [P, 2, 512], F32)) for i in range(DRING // 2)]
        pr = [es.enter_context(nc.psum_tensor(f"pr{i}", [P, 512], F32)) for i in range(RING)]
        po = es.enter_context(nc.psum_tensor("po", [P, 512], F32))

        def bank(pos):
            return pd[(pos % DRING) // 2][:, pos % 2, :]

        def split_tile(q, part, rows, cols):
            return QK[0:rows, 2 * (q % QK_RING) + part, 0:cols]

        scr = {k: nc.dram_tensor("scr_" + k, (H, ROWS, JP if k == "k2" else T), F32,
                                 kind="Internal").ap() for k in ("q1", "k1", "q2", "k2")}

        zeroed = sem("zeroed")
        consts = sem("consts")
        scratch_set = sem("scratch_set")
        identr_set = sem("identr_set")
        x_copied = sem("x_copied")
        w_first = sem("w_first")
        w_rest = sem("w_rest")
        x_in = sem("x_in")
        ctx_loaded = sem("ctx_loaded")
        wff1_in = [sem(f"wff1_in{i}") for i in range(2)]
        bank_ready = sem("bank_ready")
        bank_free = sem("bank_free")
        slot_ready = sem("slot_ready")
        slot_free = sem("slot_free")
        high_ready = sem("high_ready")
        stored = [sem(f"stored{i}") for i in range(QK_RING)]
        stats_done = sem("stats_done")
        mean_done = sem("mean_done")
        var_done = sem("var_done")
        rstd_done = sem("rstd_done")
        norm_done = sem("norm_done")
        bias_done = sem("bias_done")
        staged = [sem(f"staged{par}") for par in range(2)]
        vals_staged = sem("vals_staged")
        keys_done = sem("keys_done")
        sums_out = sem("sums_out")
        max_steps = sem("max_steps")
        h_high = sem("h_high")
        h_low = sem("h_low")
        w_high = sem("w_high")
        w_low = sem("w_low")
        gate_done = sem("gate_done")
        x_stored = sem("x_stored")
        passed = sem("passed")

        block = es.enter_context(nc.Block())

        def alone(eng):
            eng.sem_inc(passed, 1)

        def pairs(eng, group):
            with eng.Fori(0, G // 2) as i:
                group(i * 2, 0)
                group(i * 2 + 1, 1)
            group(G - 1, 0)

        W_FIRST, W_REST = 3, 5

        cleared = [hT[:, :, :], VS[:, :, :, :, :], QS[:, :, :, :].bitcast(F32), MS[:, :, :, :].bitcast(F32),
                    V_uT[:, :], ident[:, :], sel[:, :]]
        CONSTS = 6

        @block.sync
        def _(sp):
            sp.dma_start(out.rearrange("b (s p) d -> (b s) (p d)", p=32),
                         x.rearrange("b (s p) d -> (b s) (p d)", p=32)).then_inc(x_copied, 16)
            for s in stored:
                sp.sem_inc(s, 16 * STORE_DMAS)
            sp.sem_inc(x_stored, 16)
            sp.wait_ge(x_copied, 16)
            sp.wait_ge(consts, CONSTS)
            ones = CT[0:2, :, :].rearrange("p t (a c) -> p a (t c)", a=1)
            zeros = V_uT[0:DH, :].rearrange("p (a n) -> p a n", a=1)
            for k in scr:
                n = scr[k].shape[2]
                for r, src, rows in ((MAX_ROW, zeros, DH),) if k[0] == "q" else (
                        (MAX_ROW, ones, 2), (MAX_ROW + 2, zeros, DH - 2)):
                    sp.dma_start(scr[k][:, r:r + rows, :].rearrange("h r n -> r h n"),
                                 src[0:rows, :, 0:n].to_broadcast([rows, H, n])).then_inc(scratch_set, 16)
            sp.wait_ge(scratch_set, 16 * 6)

            def load_entry(b):
                full = (JT - 1) * P
                sp.dma_start(XN[:, :, :], out[bass.ds(b, 1)].rearrange("b (t p) d -> p (b t) d", p=P)
                             ).then_inc(x_in, 16)
                sp.dma_start(CT[:, 0:JT - 1, :], ctx_in[bass.ds(b, 1), 0:full, :].rearrange(
                    "b (t p) c -> p (b t) c", p=P)).then_inc(ctx_loaded, 16)
                sp.dma_start(CT[0:J - full, JT - 1, :], ctx_in[bass.ds(b, 1), full:J, :].rearrange(
                    "b p c -> (b p) c")).then_inc(ctx_loaded, 16)

            load_entry(0)
            with sp.Fori(0, L) as l:
                def load(dst, name, loaded):
                    n = len(w[name].shape) - 2
                    sp.dma_start(dst, w[name][bass.ds(l, 1)].rearrange(
                        "l p " + "abcd"[:n].replace("", " ") + " -> (l p) " + "abcd"[:n].replace("", " "))
                        ).then_inc(loaded, 16)

                load(gcol[:, :, :, :], "gains", w_first)
                load(w3[:, :, :, :], "qkv1", w_first)
                sp.dma_start(brow[:, :, :].rearrange("p i n -> p (i n)"), w["biases"][bass.ds(l, 1), :].partition_broadcast(P)
                             ).then_inc(w_first, 16)
                load(wo12[:, :, :, :], "o", w_rest)
                load(w_kv2[:, :, :, :], "kv2", w_rest)
                load(w_q2[:, :, :], "q2", w_rest)
                load(b1col[:, :, :], "ff_b1", w_rest)
                load(wff2[:, :, :], "ff_w2", w_rest)
                with sp.Fori(0, B) as b:
                    it = l * B + b
                    entry = out[bass.ds(b, 1)].rearrange("b (t p) d -> p (b t) d", p=P)
                    def store(kind, jobs):
                        for i, (c, n0, cols) in enumerate(jobs):
                            q, (r, m) = QK0[kind] + i, DC[c]
                            sp.wait_ge(bank_free, it * BANKS + DRING + done(kind, i))
                            for k, part in enumerate(STACK[kind[0]]):
                                sp.dma_start(scr[kind][r // DH:(r + m) // DH, STACK_ROW[k]:STACK_ROW[k] + DH, n0:n0 + cols],
                                             split_tile(q, part, m, cols)).then_inc(stored[q % QK_RING], 16)

                    def wait_stored(tiles):
                        for s in range(QK_RING):
                            n = (tiles - s + QK_RING - 1) // QK_RING
                            sp.wait_ge(stored[s], it * (16 * STORE_DMAS * QK_TILES // QK_RING) + 16 * STORE_DMAS * (1 + n))
                            alone(sp)

                    def stage_keys(a, g, par, ks):
                        keys = ks[bass.ds(g * HG, HG), :, :]
                        sp.dma_start(KS[:, par, :, 0:a.keys].bitcast(F32),
                                     keys.rearrange("(b e) r n -> (e r) b n", e=2)).then_inc(staged[par], 16)

                    def stage_queries(g, par, qs):
                        for e in range(2):
                            sp.dma_start(QS[64 * e:64 * e + ROWS, par, e::2, :].bitcast(F32),
                                         qs[bass.ds(g * HG + e, HG // 2, 2), :, :].rearrange("h r n -> r h n")
                                         ).then_inc(staged[par], 16)

                    def attention(a, qs, ks):
                        def group(g, par):
                            sp.wait_ge(slot_ready, it * SLOTS + g * a.slots + (a.scored + 1))
                            stage_keys(a, g, par, ks)
                            stage_queries(g, par, qs)

                        with sp.Fori(0, G // 2) as i:
                            group(i * 2 + 1, 1)
                            group(i * 2 + 2, 0)

                    def load_ff1(m, a):
                        sp.dma_start(wff1[:, a, :, :, :].rearrange("p c v n -> p (c v n)"),
                                     w["ff_w1"][bass.ds(l, 1), bass.ds(m, 1), :, :].rearrange(
                                         "l m p n -> (l m p) n")).then_inc(wff1_in[a], 16)

                    store("q1", ROW_JOBS)
                    store("k1", ROW_JOBS)
                    wait_stored(QK0["k2"])
                    stage_keys(SELF, 0, 0, scr["k1"])
                    stage_queries(0, 0, scr["q1"])
                    attention(SELF, scr["q1"], scr["k1"])
                    store("k2", KEY_JOBS)
                    wait_stored(QK0["q2"])
                    stage_keys(CROSS, 0, 0, scr["k2"])
                    store("q2", ROW_JOBS)
                    wait_stored(QK_TILES)
                    stage_queries(0, 0, scr["q2"])
                    sp.wait_ge(bias_done, it * (3 * TT) + TT)
                    alone(sp)
                    sp.wait_ge(bank_free, it * BANKS + DRING + done("tc"))
                    alone(sp)
                    load_entry((b + 1) % B)
                    for a in range(2):
                        load_ff1(a, a)
                    attention(CROSS, scr["q2"], scr["k2"])
                    with sp.Fori(0, FM // 2 - 1) as i:
                        for a in range(2):
                            m = i * 2 + a
                            sp.wait_ge(w_low, it * FM + m + 1)
                            load_ff1(m + 2, a)
                    sp.wait_ge(bank_free, it * BANKS + DRING + BANKS)
                    sp.dma_start(entry, X[:, :, :]).then_inc(x_stored, 16)
                    sp.wait_ge(x_stored, it * 16 + 32)
                    alone(sp)
            sp.wait_ge(x_in, 16 * (L * B + 1))
            sp.wait_ge(ctx_loaded, 32 * (L * B + 1))

        @block.gpsimd
        def _(pool):
            gp = nc.gpsimd
            for t in cleared:
                gp.memset(t, 0.0).then_inc(zeroed, 1)
            pool.sem_inc(vals_staged, 1)
            gp.memset(minus_half[:, :], -0.5).then_inc(consts, 1)
            gp.memset(OU[:, :], 1.0).then_inc(consts, 1)
            gp.memset(CT[:, :, :], 1.0).then_inc(consts, 1)
            pool.wait_ge(zeroed, len(cleared))
            gp.affine_select(out=ident[:, :], in_=ident[:, :], compare_op=ALU.not_equal, fill=1.0,
                             base=0, pattern=[[-1, P]], channel_multiplier=1).then_inc(consts, 1)
            of_head = sel[:, :].rearrange("p (a m) -> p a m", a=HG)
            gp.affine_select(out=of_head, in_=of_head, compare_op=ALU.not_equal, fill=1.0,
                             base=-DH, pattern=[[-32, HG], [0, 32]], channel_multiplier=1).then_inc(consts, 1)
            gp.memset(VS[:, :, :, :, DH:DH + 1], 1.0).then_inc(consts, 1)
            with pool.Fori(0, L) as l:
                pool.wait_ge(w_first, l * (16 * W_FIRST) + 16 * W_FIRST)
                alone(pool)
                with pool.Fori(0, B) as b:
                    it = l * B + b

                    def norm_scale(i):
                        pool.wait_ge(mean_done, it * (3 * TT) + TT * (i + 1))
                        alone(pool)
                        gp.tensor_scalar(rstd[:, 0, :], mv[:, :, 1], EPS, None, ALU.add).then_inc(var_done, 1)
                        pool.wait_ge(var_done, it * 3 + i + 1)
                        gp.tensor_tensor(rstd[:, 1, :], rstd[:, 0, :], minus_half[:, :], ALU.pow
                                         ).then_inc(rstd_done, 1)
                        pool.wait_ge(norm_done, it * (3 * TT) + TT * (i + 1))
                        if i == 0:
                            pool.wait_ge(x_stored, it * 16 + 16)
                        for t in range(TT):
                            gp.tensor_tensor(X[:, t, :], (X if i else XN)[:, t, :], brow[:, i, :], ALU.add
                                             ).then_inc(bias_done, 1)

                    def attention(a, stage):
                        def stage_values(g, par):
                            pool.wait_ge(keys_done, it * KTS + g * a.kt + (KT_CREDIT + a.kt0 - a.kt))
                            alone(pool)
                            for k in range(0, a.kt, 4):
                                n = min(4, a.kt - k)
                                ins = gp.tensor_copy(VS[:, par, k:k + n, :, 0:DH],
                                                     V[:, k:k + n, bass.ds(g * (HG * DH), HG * DH)].rearrange(
                                                         "p k (h d) -> p k h d", h=HG))
                            ins.then_inc(vals_staged, 1)

                        pool.wait_ge(bank_free, it * BANKS + DRING + done(stage))
                        alone(pool)
                        pairs(pool, stage_values)

                    norm_scale(0)
                    attention(SELF, "v1")
                    norm_scale(1)
                    attention(CROSS, "v2")
                    norm_scale(2)

        @block.scalar
        def _(act):
            act.sem_inc(slot_free, RING)
            act.sem_inc(sums_out, 1)
            with act.Fori(0, L) as l:
                with act.Fori(0, B) as b:
                    it = l * B + b

                    def high(kind, jobs, scale):
                        for i, (c, n0, cols) in enumerate(jobs):
                            q, m = QK0[kind] + i, DC[c][1]
                            act.wait_ge(bank_ready, it * BANKS + done(kind, i))
                            act.wait_ge(stored[q % QK_RING], it * (16 * STORE_DMAS * QK_TILES // QK_RING) + 16 * STORE_DMAS * (1 + q // QK_RING))
                            nc.scalar.activation(split_tile(q, 0, m, cols).bitcast(F32R),
                                                 bank(POS[kind] + i)[0:m, 0:cols], ACT.Copy, scale=scale
                                                 ).then_inc(high_ready, 1)

                    def attention(a):
                        def turn(par, r, slot):
                            for pair in range(2):
                                act.wait_ge(slot_ready, it * SLOTS + slot + (pair + 2))
                                for e in range(2):
                                    row = 64 * e + MAX_ROW
                                    ins = nc.scalar.copy(QS[row:row + 2, par, 2 * pair + e, :],
                                                         pr[(r + pair) % RING][row:row + 2, :])
                                ins.then_inc(slot_free, 1)

                        def group(g, par, last=False):
                            r, slot = 2, g * a.slots + a.first
                            for k, m in enumerate(a.key_rows):
                                act.wait_ge(keys_done, it * KTS + g * a.kt + (a.kt0 + k + KT_CREDIT - 1))
                                for h in range(HG):
                                    act.wait_ge(slot_ready, it * SLOTS + slot + 2)
                                    nc.scalar.activation(ET[0:m, (par * a.kt + k) % 2, h, :], pr[r % RING][0:m, :],
                                                         ACT.Exp).then_inc(slot_free, 1)
                                    r, slot = r + 1, slot + 1
                                if k == a.mt_at and not last and not a.mt_last:
                                    turn(1 - par, r, slot)
                                    r, slot = r + 2, slot + 2
                            act.wait_ge(keys_done, it * KTS + g * a.kt + (a.kt0 + a.kt + KT_CREDIT))
                            divided = 4 if last else 2 * (a.spread_at + 1)
                            act.wait_ge(bank_free, it * BANKS + a.bank_at(g) + (divided + DRING))
                            nc.scalar.copy(OU[:, :], po[:, :]).then_inc(sums_out, 1)
                            if a.mt_last and not last:
                                turn(1 - par, r, slot)

                        turn(0, 0, a.slot0)
                        with act.Fori(0, G // 2) as i:
                            group(i * 2, 0)
                            group(i * 2 + 1, 1)
                        group(G - 1, 0, last=True)

                    high("q1", ROW_JOBS, DH ** -0.5)
                    high("k1", ROW_JOBS, 1.0)
                    attention(SELF)
                    high("k2", KEY_JOBS, 1.0)
                    high("q2", ROW_JOBS, DH ** -0.5)
                    attention(CROSS)

                    def split_w(m, j, i):
                        act.wait_ge(wff1_in[j], it * (16 * (FM // 2)) + i * 16 + 16)
                        nc.scalar.copy(WS[:, j, 0], wff1[:, j]).then_inc(w_high, 1)

                    for j in range(2):
                        split_w(j, j, 0)
                    for c in range(KC):
                        act.wait_ge(bank_free, it * BANKS + (DRING + done("t3", c)))
                        nc.scalar.copy(HS[:, 0, c, :], hT[:, c, :]).then_inc(h_high, 1)
                    act.wait_ge(w_rest, l * (16 * W_REST) + 16 * W_REST)
                    alone(act)

                    def gates(i, j, last=False):
                        m = i * 2 + j
                        act.wait_ge(bank_ready, it * BANKS + m * 2 + (POS["ff1"] + 1))
                        act.wait_ge(bank_free, it * BANKS + m * 2 + (POS["ff1"] + DRING - 2))
                        nc.scalar.activation(ET[:, 0, j, :], bank(2 * j), ACT.Gelu,
                                             bias=b1col[:, 1, bass.ds(m, 1)]).then_inc(gate_done, 1)
                        if not last:
                            act.wait_ge(bank_ready, it * BANKS + m * 2 + (POS["ff1"] + 2))
                            alone(act)
                            split_w(m + 2, j, i + 1)

                    with act.Fori(0, FM // 2 - 1) as i:
                        for j in range(2):
                            gates(i, j)
                    for j in range(2):
                        gates(FM // 2 - 1, j, last=True)

        @block.vector
        def _(dve):
            v = nc.vector
            dve.sem_inc(bank_free, DRING)
            dve.wait_ge(consts, CONSTS)
            v.tensor_copy(identr[:, :], ident[:, :]).then_inc(identr_set, 1)
            with dve.Fori(0, L) as l:
                dve.wait_ge(w_first, l * (16 * W_FIRST) + 16 * W_FIRST)
                alone(dve)
                with dve.Fori(0, B) as b:
                    it = l * B + b

                    def measure(i):
                        src = X if i else XN
                        for t in range(TT):
                            v.bn_stats(stats[:, t, :], src[:, t, :]).then_inc(stats_done, 1)
                        for t in range(TT):
                            dve.wait_ge(stats_done, it * (3 * TT) + TT * i + t + 1)
                            alone(dve)
                            v.bn_aggr(mv[:, t, :], stats[:, t, :]).then_inc(mean_done, 1)

                    def normalise(i):
                        src = X if i else XN
                        dve.wait_ge(rstd_done, it * 3 + i + 1)
                        for t in range(TT):
                            v.tensor_scalar(HN[:, t, :], src[:, t, :], mv[:, t, 0:1], rstd[:, 1, t:t + 1],
                                            ALU.subtract, ALU.mult).then_inc(norm_done, 1)

                    def gain(i):
                        stage = f"t{i + 1}"
                        for c, (r, m) in enumerate(DC):
                            dve.wait_ge(bank_ready, it * BANKS + done(stage, c))
                            v.tensor_scalar(hT[0:m, c, :], bank(POS[stage] + c)[0:m, :], gcol[0:m, i, 0, c:c + 1],
                                            gcol[0:m, i, 1, c:c + 1], ALU.mult, ALU.add
                                            ).then_inc(bank_free, step(stage, c))

                    def low(kind, jobs, scale):
                        for i, (c, n0, cols) in enumerate(jobs):
                            q, m = QK0[kind] + i, DC[c][1]
                            dve.wait_ge(high_ready, it * QK_TILES + q + 1)
                            v.scalar_tensor_tensor(split_tile(q, 1, m, cols), bank(POS[kind] + i)[0:m, 0:cols],
                                                   scale, split_tile(q, 0, m, cols), ALU.mult, ALU.subtract
                                                   ).then_inc(bank_free, step(kind, i))

                    def take_values(stage, rows, groups):
                        dve.wait_ge(vals_staged, it * GROUPS + groups + 1)
                        for k, m in enumerate(rows):
                            dve.wait_ge(bank_ready, it * BANKS + done(stage, k))
                            v.tensor_copy(V[0:m, k, :], bank(POS[stage] + k)[0:m, 0:D]
                                          ).then_inc(bank_free, step(stage, k))

                    def attention(a):
                        def reduce(u, at, i):
                            h, qts, n0, cols = a.units[u]
                            dve.wait_ge(bank_ready, it * BANKS + at + (2 * i + 2))
                            both = pd[i % 2]
                            if a is SELF:
                                v.reduce_max(mx[:, qts[0]:qts[0] + 2, h, 0], both[:, :, 0:cols], AX_X
                                             ).then_inc(bank_free, 2)
                            else:
                                v.reduce_max(mx[:, qts[0], h, n0 // HALF:n0 // HALF + 1],
                                             both[:, :, :].rearrange("p a n -> p (a n)")[:, 0:cols], AX_X
                                             ).then_inc(bank_free, 2)

                        def minus_maxima(g, end):
                            dve.wait_ge(bank_free, it * BANKS + end + DRING)
                            by_pair = nm[:, :, :].rearrange("p t (b e) -> p t b e", e=2)
                            v.tensor_reduce(nm[:, :, :], mx[:, :, :, 0:1 if a is SELF else 2], AX_X, ALU.max,
                                            negate=True).then_inc(max_steps, 1)
                            dve.wait_ge(max_steps, it * (3 * GROUPS) + g * 3 + (3 * a.num0 + 1))
                            v.tensor_copy(MS[:, :, :, MAX_ROW::64], by_pair).then_inc(max_steps, 1)
                            dve.wait_ge(max_steps, it * (3 * GROUPS) + g * 3 + (3 * a.num0 + 2))
                            v.tensor_tensor(MS[:, :, :, MAX_ROW + 1::64], by_pair,
                                            MS[:, :, :, MAX_ROW::64].bitcast(F32), ALU.subtract
                                            ).then_inc(max_steps, 1)

                        def invert(at, i):
                            dve.wait_ge(bank_ready, it * BANKS + at + (2 * i + 2))
                            v.reciprocal(RD[:, :, :].rearrange("p t h -> p (t h)"), pd[i % 2][:, 0, 0:TT * HG]
                                         ).then_inc(bank_free, 2)

                        def divide(g, at, i):
                            dve.wait_ge(bank_ready, it * BANKS + at + (2 * i + 2))
                            dst = OA[:, G, :] if g is G else OA[:, bass.ds(g, 1), :].rearrange("p g n -> p (g n)")
                            v.tensor_tensor(dst, pd[i % 2][:, 0, :], OU[:, :], ALU.mult).then_inc(bank_free, 2)

                        for u in range(len(a.units)):
                            reduce(u, POS[a.stage], u)
                        minus_maxima(0, done(a.stage, len(a.units) - 1))
                        with dve.Fori(0, G - 1) as g:
                            at, u = a.bank_at(g), 0
                            for i, (_, _, kind) in enumerate(a.pieces):
                                if kind == "turn":
                                    invert(at, i)
                                elif kind == "spread":
                                    divide(g, at, i)
                                else:
                                    reduce(u, at, i)
                                    u += 1
                            minus_maxima(g + 1, at + 2 * len(a.pieces))
                        for g in (G - 1, G):
                            at = a.bank_at(G - 1) + 4 * (g - (G - 1))
                            invert(at, 0)
                            divide(g, at, 1)

                    def add_to_x(stage, biases):
                        for t in range(TT):
                            dve.wait_ge(bias_done, it * (3 * TT) + TT * biases + t + 1)
                            dve.wait_ge(bank_ready, it * BANKS + done(stage, t))
                            v.tensor_tensor(X[:, t, :], bank(POS[stage] + t)[:, 0:D], X[:, t, :], ALU.add
                                            ).then_inc(bank_free, step(stage, t))
                        dve.wait_ge(bank_free, it * BANKS + DRING + done(stage))
                        alone(dve)

                    dve.wait_ge(x_in, it * 16 + 16)
                    measure(0)
                    normalise(0)
                    gain(0)
                    low("q1", ROW_JOBS, DH ** -0.5)
                    low("k1", ROW_JOBS, 1.0)
                    take_values("v1", SELF.key_rows, 0)
                    attention(SELF)
                    add_to_x("o1", 0)
                    measure(1)
                    for c in range(2):
                        for i, (n0, cols) in enumerate(JN):
                            j = c * len(JN) + i
                            dve.wait_ge(bank_ready, it * BANKS + done("tc", j))
                            if n0 + cols > J:
                                v.tensor_copy(cT[:, c, J:JP], bank(POS["tc"] + j)[0:CC, J - 1 - n0:J - n0])
                                cols = J - n0
                            v.tensor_copy(cT[:, c, n0:n0 + cols], bank(POS["tc"] + j)[0:CC, 0:cols]
                                          ).then_inc(bank_free, step("tc", j))
                    normalise(1)
                    low("k2", KEY_JOBS, 1.0)
                    gain(1)
                    low("q2", ROW_JOBS, DH ** -0.5)
                    take_values("v2", CROSS.key_rows, G)
                    attention(CROSS)
                    add_to_x("o2", 1)
                    measure(2)

                    def split_w(m, j):
                        dve.wait_ge(w_high, it * FM + m + 1)
                        v.tensor_tensor(WS[:, j, 1], wff1[:, j], WS[:, j, 0].bitcast(F32), ALU.subtract
                                        ).then_inc(w_low, 1)

                    for j in range(2):
                        split_w(j, j)
                    normalise(2)
                    gain(2)
                    for c in range(KC):
                        dve.wait_ge(h_high, it * KC + c + 1)
                        v.tensor_tensor(HS[:, 1, c, :], hT[:, c, :], HS[:, 0, c, :].bitcast(F32), ALU.subtract
                                        ).then_inc(h_low, 1)
                    dve.wait_ge(w_rest, l * (16 * W_REST) + 16 * W_REST)
                    alone(dve)

                    def gated(i, j, last=False):
                        m = i * 2 + j
                        dve.wait_ge(bank_ready, it * BANKS + m * 2 + (POS["ff1"] + 2))
                        dve.wait_ge(gate_done, it * FM + m + 1)
                        v.scalar_tensor_tensor(uT[:, bass.ds(m, 1), :].rearrange("p m n -> p (m n)"),
                                               bank(2 * j + 1), b1col[:, 0, bass.ds(m, 1)], ET[:, 0, j, :],
                                               ALU.add, ALU.mult).then_inc(bank_free, 2)
                        if not last:
                            split_w(m + 2, j)

                    with dve.Fori(0, FM // 2 - 1) as i:
                        for j in range(2):
                            gated(i, j)
                    for j in range(2):
                        gated(FM // 2 - 1, j, last=True)
                    add_to_x("ff2", 2)

        @block.tensor
        def _(pe):
            mm = nc.tensor.matmul
            pe.sem_inc(keys_done, KT_CREDIT)
            pe.sem_inc(slot_ready, 1)
            pe.wait_ge(zeroed, len(cleared))
            pe.wait_ge(consts, CONSTS)
            pe.wait_ge(identr_set, 1)
            with pe.Fori(0, L) as l:
                pe.wait_ge(w_first, l * (16 * W_FIRST) + 16 * W_FIRST)
                alone(pe)
                with pe.Fori(0, B) as b:
                    it = l * B + b

                    def turn_norm(i):
                        stage = f"t{i + 1}"
                        for c, (r, m) in enumerate(DC):
                            pe.wait_ge(bank_free, it * BANKS + begin(stage, c))
                            alone(pe)
                            for t in range(TT):
                                if c == 0:
                                    pe.wait_ge(norm_done, it * (3 * TT) + TT * i + t + 1)
                                ins = nc.tensor.transpose(bank(POS[stage] + c)[0:m, t * P:(t + 1) * P],
                                                          HN[:, t, r:r + m], ident[:, :])
                            ins.then_inc(bank_ready, step(stage, c))

                    def project(kind):
                        for c, (r, m) in enumerate(DC):
                            pe.wait_ge(bank_free, it * BANKS + begin(kind, c))
                            for k in range(KC):
                                ins = mm(bank(POS[kind] + c)[0:m, :], wsq[kind][:, k, r:r + m], hT[:, k, :],
                                         start=k == 0, stop=k == KC - 1)
                            ins.then_inc(bank_ready, step(kind, c))

                    def attention(a):
                        def unit(par, u, at, i):
                            h, qts, n0, cols = a.units[u]
                            pe.wait_ge(bank_free, it * BANKS + at + (2 * i + 2))
                            if a is SELF:
                                parts = [(q, j, 0, cols) for j, q in enumerate(qts)]
                            else:
                                parts = [(qts[0], 0, n0, 512), (qts[0], 1, n0 + 512, cols - 512)]
                            for q, j, n, width in parts:
                                ins = mm(pd[i % 2][:, j, 0:width], QS[:, par, h, q * P:(q + 1) * P],
                                         KS[:, par, h // 2, n:n + width], start=True, stop=True)
                            ins.then_inc(bank_ready, 2)

                        def wait_staged(i, par):
                            groups = (G + 1 - par) // 2
                            pe.wait_ge(staged[par], it * (16 * STAGE_DMAS * 2 * groups) + i * (16 * STAGE_DMAS)
                                       + 16 * STAGE_DMAS * (1 + (groups if a is CROSS else 0)))
                            alone(pe)

                        def turn_max(g, r, slot):
                            pe.wait_ge(max_steps, it * (3 * GROUPS) + g * 3 + 3 * (a.num0 + 1))
                            for pair in range(2):
                                pe.wait_ge(slot_free, it * SLOTS + slot + (pair + 1))
                                for q in range(TT):
                                    ins = mm(pr[(r + pair) % RING][0:64 + MAX_ROW + 2, q * P:(q + 1) * P],
                                             MS[:, q, pair, :], identr[:, :], start=True, stop=True)
                                ins.then_inc(slot_ready, 1)

                        def weigh(g, par, k, last):
                            m = a.key_rows[k]
                            for h in range(HG):
                                n = 4 * (k + 1) + (2 if k > a.mt_at and not last else 0)
                                if h == 0:
                                    pe.wait_ge(slot_free, it * SLOTS + g * a.slots + (a.first + n + RING))
                                ins = mm(po[32 * h:32 * h + 32, :], VS[0:m, par, k, h, :],
                                         ET[0:m, (par * a.kt + k) % 2, h, :], start=k == 0, stop=k == a.kt - 1)
                            ins.then_inc(keys_done, 1)

                        def turn_divisors(g, at, i):
                            pe.wait_ge(sums_out, it * GROUPS + g + (a.num0 + 1))
                            pe.wait_ge(bank_free, it * BANKS + at + (2 * i + 2))
                            for q in range(TT):
                                ins = mm(pd[i % 2][:, 0, q * HG:(q + 1) * HG], OU[:, q * P:(q + 1) * P], sel[:, ::32],
                                         start=True, stop=True)
                            ins.then_inc(bank_ready, 2)

                        def spread_reciprocals(at, turn_at, i):
                            pe.wait_ge(bank_free, it * BANKS + at + max(2 * turn_at + 2 + DRING, 2 * i + 2))
                            for q in range(TT):
                                for h in range(HG):
                                    ins = mm(pd[i % 2][32 * h:32 * h + 32, 0, q * P:(q + 1) * P],
                                             RD[:, q, h:h + 1].to_broadcast([P, 32]), ident[:, :],
                                             start=True, stop=True)
                            ins.then_inc(bank_ready, 2)

                        def group(i2, par, last=False):
                            g = i2 * 2 + par
                            r, slot = 2, g * a.slots + a.first
                            at = a.bank_at(g)
                            nxt = g + 1

                            def pieces(k, place):
                                for i, (at_k, at_place, kind) in enumerate(a.pieces):
                                    if (at_k, at_place) != (k, place):
                                        continue
                                    if kind == "turn":
                                        turn_divisors(g, at, 0 if last else i)
                                    elif kind == "spread":
                                        spread_reciprocals(at, 0 if last else a.turn_at, 1 if last else i)
                                    elif not last:
                                        u = [p[2] for p in a.pieces[:i]].count("unit")
                                        if u == 0:
                                            wait_staged(i2 + par, 1 - par)
                                        unit(1 - par, u, at, i)

                            for k, m in enumerate(a.key_rows):
                                for h in range(HG):
                                    if k == 0 and h % 2 == 0:
                                        pe.wait_ge(slot_free, it * SLOTS + g * a.slots + (a.turned + h // 2 + 1 + RING))
                                        alone(pe)
                                    pe.wait_ge(slot_free, it * SLOTS + slot + 1)
                                    mm(pr[r % RING][0:m, :], KS[:, par, h // 2, k * P:k * P + m], QS[:, par, h, :],
                                       start=True, stop=True).then_inc(slot_ready, 1)
                                    r, slot = r + 1, slot + 1
                                    pieces(k, h)
                                if k == 1:
                                    pe.wait_ge(vals_staged, it * GROUPS + g + (a.num0 + 2))
                                if k:
                                    weigh(g, par, k - 1, last)
                                pieces(k, 4)
                                if k == a.mt_at and not last and not a.mt_last:
                                    turn_max(nxt, r, slot)
                                    r, slot = r + 2, slot + 2
                            weigh(g, par, a.kt - 1, last)
                            if a.mt_last and not last:
                                turn_max(nxt, r, slot)
                            if last:
                                turn_divisors(G, at + 4, 0)
                                spread_reciprocals(at + 4, 0, 1)

                        wait_staged(0, 0)
                        for u in range(len(a.units)):
                            unit(0, u, POS[a.stage], u)
                        turn_max(0, 0, a.slot0)
                        pe.wait_ge(slot_free, it * SLOTS + (a.first + RING))
                        alone(pe)
                        with pe.Fori(0, G // 2) as i:
                            group(i, 0)
                            group(i, 1)
                        group(G // 2, 0, last=True)

                    def project_out(kind):
                        pe.wait_ge(bank_free, it * BANKS + (DRING + POS[kind]))
                        for t in range(TT):
                            pe.wait_ge(bank_free, it * BANKS + begin(kind, t))
                            for g in range(G):
                                ins = mm(bank(POS[kind] + t)[:, 0:D], OA[:, g + 1, t * P:(t + 1) * P], wo[kind][:, g, :],
                                         start=g == 0, stop=g == G - 1)
                            ins.then_inc(bank_ready, step(kind, t))

                    turn_norm(0)
                    pe.wait_ge(bank_free, it * BANKS + (DRING + done("t1")))
                    project("q1")
                    project("k1")
                    for t in range(TT):
                        pe.wait_ge(bank_free, it * BANKS + begin("v1", t))
                        for k in range(KC):
                            ins = mm(bank(POS["v1"] + t)[:, 0:D], hT[:, k, t * P:(t + 1) * P], wsq["v1"][:, k, :],
                                     start=k == 0, stop=k == KC - 1)
                        ins.then_inc(bank_ready, step("v1", t))
                    attention(SELF)
                    pe.wait_ge(w_rest, l * (16 * W_REST) + 16 * W_REST)
                    alone(pe)
                    project_out("o1")
                    pe.wait_ge(ctx_loaded, it * 32 + 32)
                    for c in range(2):
                        for i, (n0, cols) in enumerate(JN):
                            j = c * len(JN) + i
                            pe.wait_ge(bank_free, it * BANKS + begin("tc", j))
                            for k in range(n0 // P, min(JT, n0 // P + 4)):
                                m = CROSS.key_rows[k]
                                ins = nc.tensor.transpose(bank(POS["tc"] + j)[0:CC, k * P - n0:k * P - n0 + m],
                                                          CT[0:m, k, c * CC:(c + 1) * CC], ident[0:m, 0:m])
                            ins.then_inc(bank_ready, step("tc", j))
                    pe.wait_ge(bank_free, it * BANKS + (DRING + done("tc")))
                    for j, (c, n0, cols) in enumerate(KEY_JOBS):
                        r, m = DC[c]
                        pe.wait_ge(bank_free, it * BANKS + begin("k2", j))
                        for k in range(2):
                            ins = mm(bank(POS["k2"] + j)[0:m, 0:cols], wctx["k2"][:, k, r:r + m],
                                     cT[:, k, n0:n0 + cols], start=k == 0, stop=k == 1)
                        ins.then_inc(bank_ready, step("k2", j))
                    turn_norm(1)
                    pe.wait_ge(bank_free, it * BANKS + (DRING + done("t2")))
                    project("q2")
                    for j, m in enumerate(CROSS.key_rows):
                        pe.wait_ge(bank_free, it * BANKS + begin("v2", j))
                        for k in range(2):
                            ins = mm(bank(POS["v2"] + j)[0:m, 0:D], cT[:, k, j * P:j * P + m], wctx["v2"][:, k, :],
                                     start=k == 0, stop=k == 1)
                        ins.then_inc(bank_ready, step("v2", j))
                    attention(CROSS)
                    project_out("o2")
                    turn_norm(2)
                    pe.wait_ge(h_low, it * KC + KC)
                    alone(pe)
                    with pe.Fori(0, FM // 2) as i:
                        for j in range(2):
                            m = i * 2 + j
                            pe.wait_ge(w_low, it * FM + m + 1)
                            alone(pe)
                            pe.wait_ge(bank_free, it * BANKS + m * 2 + (POS["ff1"] + 2))
                            for side in (1, 0):
                                products = [(k, of_w, of_h) for k in range(KC) for of_w, of_h in ((0, 0), (1, 0), (0, 1))]
                                for n, (k, of_w, of_h) in enumerate(products):
                                    ins = mm(bank(2 * j + 1 - side), WS[:, j, of_w, k, side, :], HS[:, of_h, k, :],
                                             start=n == 0, stop=n == len(products) - 1)
                                ins.then_inc(bank_ready, 1)
                    pe.wait_ge(bank_free, it * BANKS + (DRING + done("ff1")))
                    for t in range(TT):
                        pe.wait_ge(bank_free, it * BANKS + begin("ff2", t))
                        for m in range(FM):
                            ins = mm(bank(POS["ff2"] + t)[:, 0:D], uT[:, m, t * P:(t + 1) * P], wff2[:, m, :],
                                     start=m == 0, stop=m == FM - 1)
                        ins.then_inc(bank_ready, step("ff2", t))


def kernel(**inputs):
    import numpy as np
    import concourse.bacc as bacc
    from concourse.bass_utils import run_bass_kernel_spmd as run

    def both(name):
        return np.stack([np.asarray(inputs[f"L{i}_xattn_{name}"]) for i in range(L)])

    def on_partitions(a):
        padded = np.zeros((L, KC * P, a.shape[2]), a.dtype)
        padded[:, :D] = a
        return padded.reshape(L, KC, P, -1).transpose(0, 2, 1, 3)

    def rows_of_heads(a):
        padded = np.zeros((L, G, HG, 32, D), a.dtype)
        padded[:, :, :, :DH] = a.reshape(L, G, HG, DH, D)
        return padded.reshape(L, G, P, D).transpose(0, 2, 1, 3)

    gains = np.stack([both(f"n{i + 1}_{k}") for i in range(3) for k in "gb"], axis=2)
    arrays = {
        "gains": on_partitions(gains).transpose(0, 1, 3, 2).reshape(L, P, 3, 2, KC),
        "qkv1": np.stack([on_partitions(both(k)) for k in ("q1", "k1", "v1")], axis=2),
        "q2": on_partitions(both("q2")),
        "biases": np.concatenate([both(k) for k in ("o1_b", "o2_b", "ff_b2")], axis=1),
        "o": np.stack([rows_of_heads(both(k + "_w")) for k in ("o1", "o2")], axis=2),
        "kv2": np.stack([both(k).reshape(L, 2, CC, D).transpose(0, 2, 1, 3) for k in ("k2", "v2")], axis=2),
        "ff_w1": on_partitions(both("ff_w1")).reshape(L, P, KC, 2, FM, P).transpose(0, 4, 1, 2, 3, 5).reshape(
            L, FM, P, KC * 2 * P),
        "ff_b1": both("ff_b1").reshape(L, 2, FM, P).transpose(0, 3, 1, 2),
        "ff_w2": both("ff_w2").reshape(L, FM, P, D).transpose(0, 2, 1, 3),
    }
    names = list(arrays)
    arrays.update(x=inputs["x"], ctx=inputs["ctx_768"])
    arrays = {f"{name}_dram": np.ascontiguousarray(a) for name, a in arrays.items()}

    nc = bacc.Bacc("TRN2", target_bir_lowering=False, num_devices=1)
    aps = {name: nc.dram_tensor(name, a.shape, mybir.dt.from_np(a.dtype), kind="ExternalInput").ap()
           for name, a in arrays.items()}
    out = nc.dram_tensor("out_dram", (B, T, D), F32, kind="ExternalOutput").ap()
    blocks_kernel(nc, aps["x_dram"], aps["ctx_dram"], {name: aps[f"{name}_dram"] for name in names}, out)
    return run(nc, [arrays], core_ids=[0]).results[0]["out_dram"]
```
